# Optimizing a Trainium2 kernel written in Bass

```python
import numpy as np
import jax
import jax.numpy as jnp

def _softmax(x, axis=-1):
    return jax.nn.softmax(x, axis=axis)

def _gelu(x):
    return jax.nn.gelu(x, approximate=True)

def _silu(x):
    return jax.nn.silu(x)

def _sigmoid(x):
    return jax.nn.sigmoid(x)

def _layernorm(x, axis=-1, eps=1e-05):
    m = jnp.mean(x, axis=axis, keepdims=True)
    v = jnp.var(x, axis=axis, keepdims=True)
    return (x - m) / jnp.sqrt(v + eps)

def _scatter_add(tgt, idx, src, axis=0):
    return tgt.at[idx].add(src)

def _segment_sum(src, seg, n):
    return jax.ops.segment_sum(src, seg, n)
kernel_name = 'mk_xattn_ffn_d1_seqx_r8_4cdfe2'

def setup_inputs(seed: int=0):
    np.random.seed(seed)
    _w = jnp.asarray

    def _rec_inputs():
        import jax
        import jax.numpy as jnp
        _rk = jax.random.key(seed)
        x = -0.0002928 + 1 * jax.random.normal(jax.random.fold_in(_rk, 1), (8, 128, 128), jnp.float32)
        _lenS = 128 - jax.random.randint(jax.random.fold_in(_rk, 7), (8,), 0, max(1, 128 // 4) + 1, jnp.int32)
        _lenS2 = 128 - jax.random.randint(jax.random.fold_in(_rk, 8), (8,), 0, max(1, 128 // 4) + 1, jnp.int32)
        _ctx_1024P = jax.random.normal(jax.random.fold_in(_rk, 11), (8, 16, 128), jnp.float32)
        _ctx_1024c = jax.random.dirichlet(jax.random.fold_in(_rk, 511), 0.3 * jnp.ones((16,), jnp.float32), (8, 128))
        _ctx_1024t = jnp.einsum('bsk,bkd->bsd', _ctx_1024c, _ctx_1024P)
        _ctx_1024t = _ctx_1024t * jax.lax.rsqrt(jnp.mean(jnp.square(_ctx_1024t)) + 1e-12) * 0.953939
        ctx_1024 = -1.39393e-06 + 0.999914 * (_ctx_1024t + 0.3 * jax.random.normal(jax.random.fold_in(_rk, 611), (8, 128, 128), jnp.float32))
        return (x, ctx_1024)
    x, ctx_1024 = _rec_inputs()

    def _L0_xattn_setup():
        import jax, jax.numpy as jnp
        import numpy as np
        B, S, D, NH = (2, 256, 128, 8)
        DH = D // NH
        EPS = 1e-06
        LN_EPS = 1e-05

        def _mlstm_cell(q, k, v, igate_w, igate_b, fgate_w, fgate_b, ln_scale):
            Slen = q.shape[0]
            ifg = jnp.concatenate([q, k, v], axis=-1)
            ig = (ifg @ igate_w.T + igate_b).T
            fg = (ifg @ fgate_w.T + fgate_b).T
            qh = q.reshape(Slen, NH, DH).transpose(1, 0, 2)
            kh = k.reshape(Slen, NH, DH).transpose(1, 0, 2)
            vh = v.reshape(Slen, NH, DH).transpose(1, 0, 2)
            log_f = jax.nn.log_sigmoid(fg)
            cs = jnp.cumsum(log_f, axis=1)
            fg_mat = cs[:, :, None] - cs[:, None, :]
            mask = jnp.tril(jnp.ones((Slen, Slen), dtype=bool))
            log_fg_mat = jnp.where(mask, fg_mat, -jnp.inf)
            log_D = log_fg_mat + ig[:, None, :]
            max_log_D = jnp.max(log_D, axis=-1, keepdims=True)
            D_mat = jnp.exp(log_D - max_log_D)
            qk = jnp.einsum('hsd,htd->hst', qh, kh) / np.sqrt(DH)
            C = qk * D_mat
            normalizer = jnp.maximum(jnp.abs(C.sum(axis=-1, keepdims=True)), jnp.exp(-max_log_D))
            h = jnp.einsum('hst,htd->hsd', C / (normalizer + EPS), vh)
            h = h.transpose(1, 0, 2).reshape(Slen, D)
            mu = h.mean(axis=-1, keepdims=True)
            var = h.var(axis=-1, keepdims=True)
            return (h - mu) / jnp.sqrt(var + LN_EPS) * ln_scale
        key = jax.random.key(seed)
        ks = jax.random.split(key, 8)
        rnd = lambda k, sh, s=1.0: jax.random.normal(k, sh, dtype=jnp.float32) * s
        return {'q': rnd(ks[0], (B, S, D)), 'k': rnd(ks[1], (B, S, D)), 'v': rnd(ks[2], (B, S, D)), 'igate_w': rnd(ks[3], (NH, 3 * D), 0.02), 'igate_b': jnp.linspace(3.0, 6.0, NH, dtype=jnp.float32), 'fgate_w': rnd(ks[4], (NH, 3 * D), 0.02), 'fgate_b': rnd(ks[5], (NH,), 0.3162278), 'ln_scale': jnp.ones((D,), dtype=jnp.float32)}
    _L0_xattn_all = _L0_xattn_setup()
    _L0_xattn_in = {k: v for k, v in _L0_xattn_all.items() if k in ('igate_w', 'igate_b', 'fgate_w', 'fgate_b', 'ln_scale')}
    del _L0_xattn_all

    def _L0_ffn_setup():
        import jax, jax.numpy as jnp
        import numpy as np
        D_MODEL = 128
        D_HIDDEN = 512
        NUM_EXPERT = 8
        TOP_K = 2
        B, N = (1, 1024)

        def _expert_mlp(x, W1, b1, W2, b2, W3, b3):
            h = jax.nn.gelu(jnp.einsum('bnd,dh->bnh', x, W1) + b1, approximate=False)
            h = jax.nn.gelu(jnp.einsum('bnh,hk->bnk', h, W2) + b2, approximate=False)
            return jnp.einsum('bnh,hd->bnd', h, W3) + b3
        key = jax.random.key(seed)
        ks = jax.random.split(key, 8)
        s1 = 1.0 / np.sqrt(D_MODEL)
        s2 = 1.0 / np.sqrt(D_HIDDEN)
        return {'x': jax.random.normal(ks[0], (B, N, D_MODEL), jnp.float32), 'expert_tokens': jax.random.normal(ks[1], (NUM_EXPERT, D_MODEL), jnp.float32), 'W1': jax.random.normal(ks[2], (NUM_EXPERT, D_MODEL, D_HIDDEN), jnp.float32) * s1, 'b1': jnp.zeros((NUM_EXPERT, D_HIDDEN), jnp.float32), 'W2': jax.random.normal(ks[3], (NUM_EXPERT, D_HIDDEN, D_HIDDEN), jnp.float32) * s2, 'b2': jnp.zeros((NUM_EXPERT, D_HIDDEN), jnp.float32), 'W3': jax.random.normal(ks[4], (NUM_EXPERT, D_HIDDEN, D_MODEL), jnp.float32) * s2, 'b3': jnp.zeros((NUM_EXPERT, D_MODEL), jnp.float32)}
    _L0_ffn_all = _L0_ffn_setup()
    _L0_ffn_in = {k: v for k, v in _L0_ffn_all.items() if k in ('expert_tokens', 'W1', 'b1', 'W2', 'b2', 'W3', 'b3')}
    del _L0_ffn_all
    return {'x': x, 'ctx_1024': ctx_1024, 'L0_xattn_igate_w': _L0_xattn_in['igate_w'], 'L0_xattn_igate_b': _L0_xattn_in['igate_b'], 'L0_xattn_fgate_w': _L0_xattn_in['fgate_w'], 'L0_xattn_fgate_b': _L0_xattn_in['fgate_b'], 'L0_xattn_ln_scale': _L0_xattn_in['ln_scale'], 'L0_ffn_expert_tokens': _L0_ffn_in['expert_tokens'], 'L0_ffn_W1': _L0_ffn_in['W1'], 'L0_ffn_b1': _L0_ffn_in['b1'], 'L0_ffn_W2': _L0_ffn_in['W2'], 'L0_ffn_b2': _L0_ffn_in['b2'], 'L0_ffn_W3': _L0_ffn_in['W3'], 'L0_ffn_b3': _L0_ffn_in['b3']}

def reference(x, ctx_1024, L0_xattn_igate_w, L0_xattn_igate_b, L0_xattn_fgate_w, L0_xattn_fgate_b, L0_xattn_ln_scale, L0_ffn_expert_tokens, L0_ffn_W1, L0_ffn_b1, L0_ffn_W2, L0_ffn_b2, L0_ffn_W3, L0_ffn_b3):
    import jax
    import jax.numpy as jnp

    def _L0_xattn_ref(q, k, v, igate_w, igate_b, fgate_w, fgate_b, ln_scale):
        import jax, jax.numpy as jnp
        import numpy as np
        B, S, D, NH = (2, 256, 128, 8)
        DH = D // NH
        EPS = 1e-06
        LN_EPS = 1e-05

        def _mlstm_cell(q, k, v, igate_w, igate_b, fgate_w, fgate_b, ln_scale):
            Slen = q.shape[0]
            ifg = jnp.concatenate([q, k, v], axis=-1)
            ig = (ifg @ igate_w.T + igate_b).T
            fg = (ifg @ fgate_w.T + fgate_b).T
            qh = q.reshape(Slen, NH, DH).transpose(1, 0, 2)
            kh = k.reshape(Slen, NH, DH).transpose(1, 0, 2)
            vh = v.reshape(Slen, NH, DH).transpose(1, 0, 2)
            log_f = jax.nn.log_sigmoid(fg)
            cs = jnp.cumsum(log_f, axis=1)
            fg_mat = cs[:, :, None] - cs[:, None, :]
            mask = jnp.tril(jnp.ones((Slen, Slen), dtype=bool))
            log_fg_mat = jnp.where(mask, fg_mat, -jnp.inf)
            log_D = log_fg_mat + ig[:, None, :]
            max_log_D = jnp.max(log_D, axis=-1, keepdims=True)
            D_mat = jnp.exp(log_D - max_log_D)
            qk = jnp.einsum('hsd,htd->hst', qh, kh) / np.sqrt(DH)
            C = qk * D_mat
            normalizer = jnp.maximum(jnp.abs(C.sum(axis=-1, keepdims=True)), jnp.exp(-max_log_D))
            h = jnp.einsum('hst,htd->hsd', C / (normalizer + EPS), vh)
            h = h.transpose(1, 0, 2).reshape(Slen, D)
            mu = h.mean(axis=-1, keepdims=True)
            var = h.var(axis=-1, keepdims=True)
            return (h - mu) / jnp.sqrt(var + LN_EPS) * ln_scale
        return jax.vmap(lambda qq, kk, vv: _mlstm_cell(qq, kk, vv, igate_w, igate_b, fgate_w, fgate_b, ln_scale))(q, k, v)

    def _L0_ffn_ref(x, expert_tokens, W1, b1, W2, b2, W3, b3):
        import jax, jax.numpy as jnp
        import numpy as np
        D_MODEL = 128
        D_HIDDEN = 512
        NUM_EXPERT = 8
        TOP_K = 2
        B, N = (1, 1024)

        def _expert_mlp(x, W1, b1, W2, b2, W3, b3):
            h = jax.nn.gelu(jnp.einsum('bnd,dh->bnh', x, W1) + b1, approximate=False)
            h = jax.nn.gelu(jnp.einsum('bnh,hk->bnk', h, W2) + b2, approximate=False)
            return jnp.einsum('bnh,hd->bnd', h, W3) + b3
        scores = jnp.einsum('bnd,ed->bne', x, expert_tokens)
        _, topk_idx = jax.lax.top_k(scores, TOP_K)
        outputs = jnp.zeros_like(x)
        num_expert = W1.shape[0]
        for i in range(num_expert):
            w = jnp.mean((topk_idx == i).astype(x.dtype), axis=-1, keepdims=True)
            y = _expert_mlp(x, W1[i], b1[i], W2[i], b2[i], W3[i], b3[i])
            outputs = outputs + y * w
        return outputs
    x = x + _L0_xattn_ref(_layernorm(x, axis=-1), ctx_1024, ctx_1024, L0_xattn_igate_w, L0_xattn_igate_b, L0_xattn_fgate_w, L0_xattn_fgate_b, L0_xattn_ln_scale)
    x = x + _L0_ffn_ref(_layernorm(x, axis=-1), L0_ffn_expert_tokens, L0_ffn_W1, L0_ffn_b1, L0_ffn_W2, L0_ffn_b2, L0_ffn_W3, L0_ffn_b3)
    return x

_drawn_inputs = setup_inputs


def setup_inputs(seed=0):
    import zlib

    import numpy as np

    out = dict(_drawn_inputs(seed))
    spreads = {'L0_xattn_ln_scale': (1.0, 0.2),
     'L0_ffn_b1': (0.0, 0.435),
     'L0_ffn_b2': (0.0, 0.291),
     'L0_ffn_b3': (0.0, 0.1)}
    factors = {}
    for name, (base, spread) in spreads.items():
        noise = np.random.default_rng([zlib.crc32(name.encode()), seed]).standard_normal(out[name].shape)
        drawn = base * np.exp(spread * noise) if base else spread * noise
        out[name] = jnp.asarray(drawn.astype(out[name].dtype))
    for name, factor in factors.items():
        out[name] = (out[name] * factor).astype(out[name].dtype)
    return out
```

```python
from collections import namedtuple
from contextlib import ExitStack

import numpy as np
import concourse.bass as bass
from concourse import mybir

F32 = mybir.dt.float32
F32R = mybir.dt.float32r
BF16 = mybir.dt.bfloat16
F16 = mybir.dt.float16
I32 = mybir.dt.int32
U32 = mybir.dt.uint32
ALU = mybir.AluOpType
ACT = mybir.ActivationFunctionType
AX = mybir.AxisListType

B, S, D = 8, 128, 128
NH = 8
DH = D // NH
BH = B * NH
NE = 8
HID = 512
MC = HID // 128
T = B * S
EPS_NORMALIZER = 1e-6
EPS_LN = 1e-5
NEG = -1e38

MAIN = 320
CHUNKS = 9
GAP = 3 * 128 - MAIN
PLACES = CHUNKS * 128
RC = 2
REST = RC * 128
PAD = 3 * 128
NC = NE * CHUNKS
STEPS = (CHUNKS - 3) // RC
WCOLS = HID + MC * HID + MC * D


def build(nc, x, ctx, igw, igb, fgw, fgb, lns, et, W1, b1, W2, b2, W3, b3, out):
    es = ExitStack()
    with es:
        def sb(name, shape, dt=F32):
            return es.enter_context(nc.sbuf_tensor(name, shape, dt))

        def sem(name):
            return es.enter_context(nc.semaphore(name))

        xnd = nc.dram_tensor("xn_rows", (T + PAD, D), F32, kind="Internal").ap()

        wraw = sb("wraw", [128, NE, WCOLS])
        whi = [sb("whi0", [128, WCOLS], F32R)]
        wlo = [sb("wlo0", [128, WCOLS], F32R)]
        identf = sb("identf", [128, 128])
        identb = sb("identb", [128, 128], BF16)
        negb = sb("negb", [128, 128], BF16)
        trib = sb("trib", [128, 128], BF16)
        onesb = sb("onesb", [128, 128], BF16)
        iota = sb("iota", [128, 128])
        iotab = sb("iotab", [128, 128], F16)
        hmask = sb("hmask", [128, NH])
        minus_half = sb("minus_half", [128, NH])
        tokval = sb("tokval", [128, B])
        padval = sb("padval", [128, NC // 3, 3])
        ebase = sb("ebase", [128, NE])
        zrow = sb("zrow", [128, D])
        ones64 = sb("ones64", [BH, S])
        onecol = sb("onecol", [128, 1])
        sm = sb("sm", [128, 128])
        smt = sb("smt", [128, 128])
        gbias = sb("gbias", [128, 1])
        lnsb = sb("lnsb", [128, D])
        ohk = sb("ohk", [128, 2, B, NE])
        maskb = sb("maskb", [128, B, NE], BF16)
        prefb = sb("prefb", [128, B + 1, NE], BF16)
        top = sb("top", [128, 2, 8])
        topi = sb("topi", [128, 2, 8], U32)
        topf = sb("topf", [128, 2, 2])
        place = sb("place", [128, BH])
        placed = sb("placed", [128, 2, B, NE])
        sl = sb("sl", [128, 2 * B])
        sli = sb("sli", [128, 2 * B], I32)
        ci = sb("ci", [128, 2 * B], I32)
        ri = sb("ri", [128, 2 * B], I32)
        cf = sb("cf", [128, 2 * B])
        rf = sb("rf", [128, 2 * B])
        padterm = sb("padterm", [128, NC])
        ids = sb("ids", [128, NC], U32)
        cntf = sb("cntf", [128, 1])
        cnti = sb("cnti", [128, 1], I32)
        rids = sb("rids", [128, RC], U32)
        rbias = sb("rbias", [128, 2 * MC + 1])
        turn = sb("turn", [128, 1])
        turnd = sb("turnd", [128, 1])

        attn = ExitStack()

        def at(name, shape, dt=F32):
            return attn.enter_context(nc.sbuf_tensor(name, shape, dt))

        xs = at("xs", [128, B, D])
        cs_in = at("cs_in", [128, B, D])
        qn = at("qn", [128, B, D])
        qT = at("qT", [128, B, S])
        cT = at("cT", [128, B, S])
        v1 = at("v1", [128, B, NH, DH + 1])
        st1 = at("st1", [128, B, 6])
        mv1 = at("mv1", [128, B, 2])
        ve1 = at("ve1", [128, B])
        rs1 = at("rs1", [128, B])
        fgt = at("fgt", [BH, S])
        nabs = at("nabs", [BH, S])
        expn = at("expn", [BH, S])
        logf = at("logf", [BH, S])
        lsum = at("lsum", [BH, S])
        u = at("u", [BH, S])
        cm = at("cm", [BH, S])
        mld = at("mld", [BH, S])
        nm = at("nm", [BH, S])
        em = at("em", [BH, S])
        emT = at("emT", [128, BH])
        parts = at("parts", [BH, 4, S], F32R)
        LT = at("LT", [18, B, S], F32R)
        RH = at("RH", [18, 2, NH, S], F32R)
        delta = at("delta", [18, NH])
        qbd = at("qbd", [128, 2, NH, S])
        dec = at("dec", [128, 2, NH, S])
        cw = dec
        den = at("den", [128, 2, NH])
        den1 = at("den1", [128, 2, NH])
        den2 = at("den2", [128, 2, NH])
        rden = at("rden", [128, 2, NH])
        hn = at("hn", [128, 2, D])
        hl = at("hl", [128, 2, D])
        st2 = at("st2", [128, 2, 6])
        mv2 = at("mv2", [128, B, 2])
        ve2 = at("ve2", [128, B])
        rs2 = at("rs2", [128, B])
        x2 = at("x2", [128, B, D])
        st3 = at("st3", [128, 2, 6])
        mv3 = at("mv3", [128, B, 2])
        ve3 = at("ve3", [128, B])
        rs3 = at("rs3", [128, B])
        xn = qn
        xnT = at("xnT", [128, 2, S])
        mark = ExitStack()
        wq = mark.enter_context(nc.sbuf_tensor("wq", [128, B * (BH * 2 + NH)], F32))
        wc = mark.enter_context(nc.sbuf_tensor("wc", [128, B * (BH * 2 + NH)], F32))
        mark.close()
        ohb = at("ohb", [128, 2 * B, 128], F16)
        oha = at("oha", [128, 2 * B, NC], F16)
        attn.close()
        whi.append(sb("whi1", [128, WCOLS], F32R))
        wlo.append(sb("wlo1", [128, WCOLS], F32R))
        xg = sb("xg", [128, 2, 3, D])
        xhi = sb("xhi", [128, MAIN], F32R)
        xlo = sb("xlo", [128, MAIN], F32R)
        g1 = sb("g1", [128, MC, MAIN])
        g1h = sb("g1h", [128, MC, MAIN], F32R)
        g1l = sb("g1l", [128, MC, MAIN], F32R)
        g2 = sb("g2", [128, MC, MAIN])
        g2h = sb("g2h", [128, MC, MAIN], F32R)
        g2l = sb("g2l", [128, MC, MAIN], F32R)
        yT = sb("yT", [128, MAIN])
        ys = sb("ys", [128, 2, 3, D])

        bank = [es.enter_context(nc.psum_tensor(f"bank{i}", [128, 512], F32)) for i in range(8)]

        names = """
        x_in0 x_in1 ctx_in0 ctx_in1 small_in ctx_small w_in0 w_in1 w_in2 w_in3 w_in4 w_in5 w_in6 w_in7
        const_zero const_done iota_done ve1_done rs1_done st1_done mv1_done qn_done sm_T smt_done
        qT_ps cT_ps qT_done cT_done wq_zero wpad_done v1_done gates_ps
        fgt_done nabs_done expn_done softplus_done logf_done lsum_done u_done cm_done mld_done nm_done em_done
        hi_done parts_done rows_in emT_ps max_in0 max_in1 emT_done delta_done rh_done lt_ones
        qbd_done qk_ps arg_ps dec_done cw_done pv_ps den1_done den_done den2_done rden_done hn_done st2_done mv2_done
        ve2_done rs2_done hl_done x2_done st3_done mv3_done ve3_done rs3_done xn_done xnT_ps xnT_done score_ps
        top_done topi_done topf_done oh_done mask_done pref_done rank_ps ge_done place_done base_done placed_done
        sl_done sli_done split_done splitf_done oha_done lists_ps padterm_done ids_done cnt_done cnti_done
        xn_out x2_out gathered0 gathered1 whi_done wlo_done xT_ps xhi_done xlo_done l1_ps gelu1_done g1h_done g1l_done
        l2_ps gelu2_done g2h_done g2l_done l3_ps yT_done y_ps ys_done added
        r_turn r_whi r_wlo r_ids r_bias r_gathered r_xT r_xhi r_xlo r_l1 r_gelu1 r_g1h r_g1l
        r_l2 r_gelu2 r_g2h r_g2l r_l3 r_yT r_y r_ys r_added
        """.split()
        s = namedtuple("Semaphores", names)(*[sem(n) for n in names])
        x_in = [s.x_in0, s.x_in1]
        ctx_in = [s.ctx_in0, s.ctx_in1]
        max_in = [s.max_in0, s.max_in1]
        gathered = [s.gathered0, s.gathered1]
        w_in = [s.w_in0, s.w_in1, s.w_in2, s.w_in3, s.w_in4, s.w_in5, s.w_in6, s.w_in7]

        def wcol(w, p, layer, k, m):
            at_ = {1: 0, 2: HID, 3: HID + MC * HID}[layer]
            width = D if layer == 3 else HID
            c = at_ + k * width + m * 128
            return w[p][:, c:c + 128]

        def most_tokens(engine):
            engine.wait_ge(s.cnti_done, 1)
            return engine.value_load(cnti[0:1, 0:1], min_val=0, max_val=T)

        def qk_bank(b, half):
            return bank[(2 * b + half) % 3]

        arg_bank = bank[3:5]
        pv_bank = bank[5:7]
        misc = bank[7]

        block = es.enter_context(nc.Block())

        @block.sync
        def _(sp):
            half = B // 2
            for i in range(2):
                sp.dma_start(xs[:, i * half:(i + 1) * half, :],
                             x[i * half:(i + 1) * half].rearrange("b s d -> s b d")).then_inc(x_in[i], 16)
                sp.dma_start(cs_in[:, i * half:(i + 1) * half, :],
                             ctx[i * half:(i + 1) * half].rearrange("b s d -> s b d")).then_inc(ctx_in[i], 16)
            for e in range(NE):
                sp.dma_start(wraw[:, e, 0:HID], W1[e]).then_inc(w_in[e], 16)
                sp.dma_start(wraw[:, e, HID:HID + MC * HID].rearrange("p (k n) -> p k n", k=MC),
                             W2[e].rearrange("(k p) n -> p k n", p=128)).then_inc(w_in[e], 16)
                sp.dma_start(wraw[:, e, HID + MC * HID:].rearrange("p (k n) -> p k n", k=MC),
                             W3[e].rearrange("(k p) n -> p k n", p=128)).then_inc(w_in[e], 16)

            sp.wait_ge(s.const_zero, 13)
            zeros = zrow[:].unsqueeze(1).to_broadcast([128, PAD // 128, D])
            sp.dma_start(xnd[T:T + PAD, :].rearrange("(c p) d -> p c d", p=128), zeros).then_inc(s.xn_out, 16)
            sp.dma_start(out[T:T + PAD, :].rearrange("(c p) d -> p c d", p=128), zeros).then_inc(s.x2_out, 16)
            for b in range(B):
                sp.wait_ge(s.x2_done, b + 1)
                sp.dma_start(out[b * S:(b + 1) * S, :], x2[:, b, :]).then_inc(s.x2_out, 16)
                sp.wait_ge(s.xn_done, b + 1)
                sp.dma_start(xnd[b * S:(b + 1) * S, :], xn[:, b, :]).then_inc(s.xn_out, 16)

        @block.gpsimd
        def _(pool):
            g = nc.gpsimd
            g.memset(wq[:], 0.0).then_inc(s.wq_zero, 1)
            g.memset(wc[:], 0.0).then_inc(s.wq_zero, 1)
            g.memset(identf[:], 0.0).then_inc(s.const_zero, 1)
            g.memset(hmask[:], 0.25).then_inc(s.const_zero, 1)
            g.memset(minus_half[:], -0.5).then_inc(s.const_zero, 1)
            g.memset(identb[:], 0.0).then_inc(s.const_zero, 1)
            g.memset(negb[:], NEG).then_inc(s.const_zero, 1)
            g.memset(trib[:], 1.0).then_inc(s.const_zero, 1)
            g.memset(onesb[:], 1.0).then_inc(s.const_zero, 1)
            g.memset(delta[:], 0.0).then_inc(s.const_zero, 1)
            g.memset(zrow[:], 0.0).then_inc(s.const_zero, 1)
            g.memset(ones64[:], 1.0).then_inc(s.const_zero, 1)
            g.memset(onecol[:], 1.0).then_inc(s.const_zero, 1)
            g.memset(prefb[:, 0, :], 0.0).then_inc(s.const_zero, 1)
            g.memset(v1[:, :, :, DH:DH + 1], 1.0).then_inc(s.const_zero, 1)
            g.memset(LT[:].bitcast(F32), 1.0).then_inc(s.lt_ones, 1)
            pool.wait_ge(s.const_zero, 13)
            g.affine_select(out=identf[:], in_=identf[:], compare_op=ALU.not_equal, fill=1.0, base=0,
                            pattern=[[-1, 128]], channel_multiplier=1).then_inc(s.const_done, 1)
            g.affine_select(out=identb[:], in_=identb[:], compare_op=ALU.not_equal, fill=1.0, base=0,
                            pattern=[[-1, 128]], channel_multiplier=1).then_inc(s.const_done, 1)
            g.affine_select(out=negb[:], in_=negb[:], compare_op=ALU.is_gt, fill=0.0, base=0,
                            pattern=[[-1, 128]], channel_multiplier=1).then_inc(s.const_done, 1)
            g.affine_select(out=trib[:], in_=trib[:], compare_op=ALU.is_gt, fill=0.0, base=0,
                            pattern=[[1, 128]], channel_multiplier=-1).then_inc(s.const_done, 1)
            g.affine_select(out=hmask[:], in_=hmask[:], compare_op=ALU.is_ge, fill=0.0, base=0,
                            pattern=[[-DH, NH]], channel_multiplier=1).then_inc(s.const_done, 1)
            pool.wait_ge(s.const_done, 5)
            g.affine_select(out=hmask[:], in_=hmask[:], compare_op=ALU.is_ge, fill=0.0, base=DH - 1,
                            pattern=[[DH, NH]], channel_multiplier=-1).then_inc(s.const_done, 1)
            g.affine_select(out=delta[:], in_=delta[:], compare_op=ALU.not_equal, fill=1.0, base=0,
                            pattern=[[-1, NH]], channel_multiplier=1).then_inc(s.const_done, 1)
            pool.wait_ge(s.const_done, 7)
            g.affine_select(out=delta[:], in_=delta[:], compare_op=ALU.not_equal, fill=1.0, base=-NH,
                            pattern=[[-1, NH]], channel_multiplier=1).then_inc(s.delta_done, 1)
            g.iota(iota[:], pattern=[[1, 128]], base=0, channel_multiplier=0,
                   allow_small_or_imprecise_dtypes=True).then_inc(s.iota_done, 1)
            g.iota(iotab[:], pattern=[[1, 128]], base=0, channel_multiplier=0,
                   allow_small_or_imprecise_dtypes=True).then_inc(s.iota_done, 1)
            g.iota(tokval[:], pattern=[[S, B]], base=-2 * T, channel_multiplier=1,
                   allow_small_or_imprecise_dtypes=True).then_inc(s.iota_done, 1)
            g.iota(padval[:], pattern=[[0, NC // 3], [128, 3]], base=-T, channel_multiplier=1,
                   allow_small_or_imprecise_dtypes=True).then_inc(s.iota_done, 1)
            g.iota(ebase[:], pattern=[[PLACES, NE]], base=0, channel_multiplier=0,
                   allow_small_or_imprecise_dtypes=True).then_inc(s.iota_done, 1)
            pool.wait_ge(ctx_in[0], 16)
            pool.wait_ge(ctx_in[1], 16)
            g.tensor_copy(v1[:, :, :, 0:DH], cs_in[:].rearrange("p b (h c) -> p b h c", c=DH)).then_inc(s.v1_done, 1)
            pool.wait_ge(s.ve1_done, 1)
            g.tensor_tensor(rs1[:], ve1[:], minus_half[:], ALU.pow).then_inc(s.rs1_done, 1)

            def make_qbd(b):
                if b >= 2:
                    pool.wait_ge(s.qk_ps, b - 1)
                g.tensor_tensor(qbd[:, b % 2, :, :], qT[:, b:b + 1, :].to_broadcast([128, NH, S]),
                                hmask[:].unsqueeze(2).to_broadcast([128, NH, S]), ALU.mult).then_inc(s.qbd_done, 1)
            pool.wait_ge(s.qT_done, 2)
            make_qbd(0)
            make_qbd(1)
            for i in range(B + 3):
                if 2 <= i < B:
                    make_qbd(i)
                if 0 <= i - 1 < B:
                    b = i - 1
                    pool.wait_ge(s.ve2_done, b + 1)
                    g.tensor_tensor(rs2[:, b:b + 1], ve2[:, b:b + 1], minus_half[:, 0:1], ALU.pow)\
                        .then_inc(s.rs2_done, 1)
                if 0 <= i - 2 < B:
                    b = i - 2
                    pool.wait_ge(s.ve3_done, b + 1)
                    g.tensor_tensor(rs3[:, b:b + 1], ve3[:, b:b + 1], minus_half[:, 0:1], ALU.pow)\
                        .then_inc(s.rs3_done, 1)

            def gather(e):
                if e >= 2:
                    pool.wait_ge(s.xT_ps, e - 1)
                for c in range(3):
                    n = min(128, MAIN - 128 * c)
                    col = CHUNKS * e + c
                    g.indirect_dma_start(out=xg[0:n, e % 2, c, :], out_offset=None, in_=xnd,
                                         in_offset=bass.IndirectOffsetOnAxis(ap=ids[0:n, col:col + 1], axis=0))\
                        .then_inc(gathered[e % 2], 16)

            def weights_lo(e):
                pool.wait_ge(s.whi_done, e + 1)
                g.tensor_tensor(wlo[e % 2][:], wraw[:, e, :], whi[e % 2][:].bitcast(F32), ALU.subtract)\
                    .then_inc(s.wlo_done, 1)

            def scatter(e):
                pool.wait_ge(s.ys_done, e + 1)
                if e >= 1:
                    pool.wait_ge(s.added, 48 * e)
                for c in range(3):
                    n = min(128, MAIN - 128 * c)
                    col = CHUNKS * e + c
                    g.indirect_dma_start(out=out, out_offset=bass.IndirectOffsetOnAxis(ap=ids[0:n, col:col + 1], axis=0),
                                         in_=ys[0:n, e % 2, c, :], in_offset=None, compute_op=ALU.add)\
                        .then_inc(s.added, 16)
            weights_lo(0)
            pool.wait_ge(s.ids_done, 1)
            pool.wait_ge(s.xn_out, 16 * (B + 1))
            pool.wait_ge(s.x2_out, 16 * (B + 1))
            gather(0)
            gather(1)
            weights_lo(1)
            for e in range(NE):
                if e >= 1 and e + 1 < NE:
                    gather(e + 1)
                    weights_lo(e + 1)
                if e >= 1:
                    scatter(e - 1)
                if e == 2:
                    most = most_tokens(pool)
            scatter(NE - 1)
            pool.wait_ge(s.added, 48 * NE)

            def tick(before=None):
                if before is not None:
                    pool.wait_ge(s.r_turn, before)
                g.tensor_tensor(turn[:], onecol[:], onecol[:], ALU.mult).then_inc(s.r_turn, 1)

            with pool.If(most > MAIN):
                tick()
                with pool.Fori(0, NE) as e:
                    pool.wait_ge(s.r_whi, e + 1)
                    g.tensor_tensor(wlo[0][:], wraw[:, bass.ds(e, 1), :].rearrange("p o w -> p (o w)"),
                                    whi[0][:].bitcast(F32), ALU.subtract).then_inc(s.r_wlo, 1)
                    for c in range(STEPS):
                        over = STEPS * e + c
                        pool.wait_ge(s.r_ids, over + 1)
                        tick(3 * over + 1)
                        for j in range(RC):
                            g.indirect_dma_start(out=xg[:, 0, j, :], out_offset=None, in_=xnd,
                                                 in_offset=bass.IndirectOffsetOnAxis(ap=rids[:, j:j + 1], axis=0))\
                                .then_inc(s.r_gathered, 16)
                        pool.wait_ge(s.r_ys, over + 1)
                        tick(3 * over + 2)
                        for j in range(RC):
                            g.indirect_dma_start(out=out, out_offset=bass.IndirectOffsetOnAxis(ap=rids[:, j:j + 1], axis=0),
                                                 in_=ys[:, 0, j, :], in_offset=None, compute_op=ALU.add)\
                                .then_inc(s.r_added, 16)
                        pool.wait_ge(s.r_added, 16 * RC * (over + 1))
                        tick(3 * over + 3)

        @block.scalar
        def _(act):
            a = nc.scalar
            for i, (src, rows) in enumerate(((b1.rearrange("e (m p) -> (e m) p", p=128), NE * MC),
                                             (b2.rearrange("e (m p) -> (e m) p", p=128), NE * MC),
                                             (b3, NE), (et, NE))):
                lo = (0, 32, 64, 72)[i]
                act.dma_start(sm[lo:lo + rows, :], src).then_inc(s.small_in, 16)
            for c in range(3):
                act.dma_start(sm[80 + 8 * c:88 + 8 * c, :], igw[:, c * D:(c + 1) * D]).then_inc(s.small_in, 16)
                act.dma_start(sm[104 + 8 * c:112 + 8 * c, :], fgw[:, c * D:(c + 1) * D]).then_inc(s.small_in, 16)
            for b in range(B):
                act.dma_start(gbias[NH * b:NH * b + NH, :], igb.rearrange("(h o) -> h o", o=1)).then_inc(s.small_in, 16)
                act.dma_start(gbias[BH + NH * b:BH + NH * b + NH, :], fgb.rearrange("(h o) -> h o", o=1))\
                    .then_inc(s.small_in, 16)
            act.dma_start(lnsb[:], lns.partition_broadcast(128)).then_inc(s.small_in, 16)
            act.wait_ge(s.delta_done, 1)
            a.activation(RH[:], delta[:].unsqueeze(1).unsqueeze(3).to_broadcast([18, 2, NH, S]), ACT.Copy).then_inc(s.rh_done, 1)
            act.wait_ge(s.qT_ps, 4)
            a.activation(qT[:, 0:4, :], arg_bank[0][:].rearrange("p (b t) -> p b t", t=S), ACT.Copy).then_inc(s.qT_done, 1)
            act.wait_ge(s.qT_ps, 8)
            a.activation(qT[:, 4:8, :], arg_bank[1][:].rearrange("p (b t) -> p b t", t=S), ACT.Copy).then_inc(s.qT_done, 1)
            act.wait_ge(s.nabs_done, 1)
            a.activation(expn[:], nabs[:], ACT.Exp).then_inc(s.expn_done, 1)
            act.wait_ge(s.expn_done, 1)
            a.activation(nabs[:], expn[:], ACT.Ln, bias=onecol[0:BH, :]).then_inc(s.softplus_done, 1)
            act.wait_ge(s.mld_done, 1)
            a.activation(em[:], mld[:], ACT.Exp, scale=-1.0).then_inc(s.em_done, 1)
            act.wait_ge(s.parts_done, 2)
            act.wait_ge(s.lt_ones, 1)
            act.wait_ge(s.rh_done, 1)
            for b in range(B):
                for q in range(2):
                    act.dma_start(LT[NH * q:NH * q + NH, b, :].bitcast(F32), parts[NH * b:NH * b + NH, q, :].bitcast(F32)).then_inc(s.rows_in, 16)

            def max_rows(b):
                for q in range(2):
                    act.dma_start(RH[2 * NH + q:2 * NH + q + 1, b % 2, :, :].bitcast(F32), parts[NH * b:NH * b + NH, 2 + q, :].bitcast(F32))\
                        .then_inc(max_in[b % 2], 16)
            max_rows(0)
            max_rows(1)
            act.wait_ge(s.emT_ps, 1)
            a.activation(emT[:], misc[:, 0:BH], ACT.Copy).then_inc(s.emT_done, 1)

            for i in range(B + 3):
                if i < B:
                    b = i
                    if b >= 2:
                        act.wait_ge(s.pv_ps, b - 1)
                    for half in range(2):
                        act.wait_ge(s.arg_ps, 2 * b + half + 1)
                        a.activation(dec[:, b % 2, half * 4:half * 4 + 4, :],
                                     arg_bank[half][:].rearrange("p (h t) -> p h t", t=S), ACT.Exp).then_inc(s.dec_done, 1)
                    if b + 2 < B:
                        max_rows(b + 2)
                if 0 <= i - 3 < B:
                    b = i - 3
                    act.wait_ge(s.xnT_ps, b + 1)
                    a.activation(xnT[:, b % 2, :], misc[:, 0:S], ACT.Copy).then_inc(s.xnT_done, 1)

            def weights_hi(e):
                act.wait_ge(w_in[e], 48)
                if e >= 2:
                    act.wait_ge(s.l3_ps, e - 1)
                a.activation(whi[e % 2][:], wraw[:, e, :], ACT.Copy).then_inc(s.whi_done, 1)

            def gelu(e, layer):
                psd, done, split, dst, col = ((s.l1_ps, s.gelu1_done, s.g1l_done, g1, 0),
                                              (s.l2_ps, s.gelu2_done, s.g2l_done, g2, 32))[layer - 1]
                for m in range(MC):
                    act.wait_ge(psd, MC * e + m + 1)
                    if e >= 1:
                        act.wait_ge(split, MC * (e - 1) + m + 1)
                    a.activation(dst[:, m, :], bank[m][:, 0:MAIN], ACT.Gelu,
                                 bias=smt[:, col + MC * e + m:col + MC * e + m + 1]).then_inc(done, 1)
            weights_hi(0)
            act.wait_ge(s.ids_done, 1)
            act.wait_ge(s.xn_out, 16 * (B + 1))
            act.wait_ge(s.x2_out, 16 * (B + 1))
            weights_hi(1)
            gelu(0, 1)
            for e in range(NE):
                if 1 <= e and e + 1 < NE:
                    weights_hi(e + 1)
                gelu(e, 2)
                if e + 1 < NE:
                    gelu(e + 1, 1)
                if e == 2:
                    most = most_tokens(act)

            with act.If(most > MAIN):
                with act.Fori(0, NE) as e:
                    act.wait_ge(s.r_turn, 3 * STEPS * e + 1)
                    a.activation(whi[0][:], wraw[:, bass.ds(e, 1), :].rearrange("p o w -> p (o w)"), ACT.Copy)\
                        .then_inc(s.r_whi, 1)
                    for c in range(STEPS):
                        for psd, done, dst, col in ((s.r_l1, s.r_gelu1, g1, 0), (s.r_l2, s.r_gelu2, g2, MC)):
                            act.wait_ge(psd, STEPS * e + c + 1)
                            for m in range(MC):
                                a.activation(dst[:, m, 0:REST], bank[m][:, 0:REST], ACT.Gelu,
                                             bias=rbias[:, col + m:col + m + 1]).then_inc(done, 1)

        @block.vector
        def _(dve):
            v = nc.vector
            for b in range(B):
                dve.wait_ge(x_in[b // 4], 16)
                v.bn_stats(st1[:, b, :], xs[:, b, :]).then_inc(s.st1_done, 1)
            for b in range(B):
                dve.wait_ge(s.st1_done, b + 1)
                v.bn_aggr(mv1[:, b, :], st1[:, b, :]).then_inc(s.mv1_done, 1)
            dve.wait_ge(s.mv1_done, B)
            v.tensor_scalar_add(ve1[:], mv1[:, :, 1], EPS_LN).then_inc(s.ve1_done, 1)
            dve.wait_ge(s.sm_T, 1)
            v.tensor_copy(smt[:], bank[0][:, 0:128]).then_inc(s.smt_done, 1)
            dve.wait_ge(s.smt_done, 1)
            dve.wait_ge(s.wq_zero, 2)
            pad = BH * 2 + NH

            def padded(w):
                return w[:].rearrange("p (b c) -> p b c", c=pad)[:, :, 0:2 * BH]\
                    .rearrange("p b (g c) -> p b g c", c=BH)[:, :, :, 0:NH]

            def gate_part(c):
                return smt[:, 80:128].rearrange("p (g c h) -> p g c h", g=2, c=3)[:, :, c, :]\
                    .unsqueeze(1).to_broadcast([128, B, 2, NH])
            for gg in range(2):
                v.tensor_copy(padded(wq)[:, :, gg, :], gate_part(0)[:, :, gg, :]).then_inc(s.wpad_done, 1)
                v.tensor_tensor(padded(wc)[:, :, gg, :], gate_part(1)[:, :, gg, :], gate_part(2)[:, :, gg, :],
                                ALU.add).then_inc(s.wpad_done, 1)
            dve.wait_ge(s.rs1_done, 1)
            for b in range(B):
                v.tensor_scalar(qn[:, b, :], xs[:, b, :], mv1[:, b, 0:1], rs1[:, b:b + 1], ALU.subtract, ALU.mult)\
                    .then_inc(s.qn_done, 1)
            for i in range(2):
                dve.wait_ge(s.cT_ps, 4 * i + 4)
                v.tensor_copy(cT[:, 4 * i:4 * i + 4, :], bank[6 + i][:].rearrange("p (b t) -> p b t", t=S))\
                    .then_inc(s.cT_done, 1)
            dve.wait_ge(s.gates_ps, 1)
            dve.wait_ge(s.small_in, 16 * 27)
            v.tensor_scalar(fgt[:], pv_bank[0][BH:128, 0:S], gbias[BH:128, :], None, ALU.add).then_inc(s.fgt_done, 1)
            dve.wait_ge(s.fgt_done, 1)
            v.scalar_tensor_tensor(out=nabs[:], in0=fgt[:], scalar=-1.0, in1=fgt[:], op0=ALU.mult, op1=ALU.min)\
                .then_inc(s.nabs_done, 1)
            dve.wait_ge(s.softplus_done, 1)
            v.scalar_tensor_tensor(out=logf[:], in0=fgt[:], scalar=0.0, in1=nabs[:], op0=ALU.min, op1=ALU.subtract)\
                .then_inc(s.logf_done, 1)
            dve.wait_ge(s.logf_done, 1)
            dve.wait_ge(s.const_zero, 13)
            v.tensor_tensor_scan(lsum[:], ones64[:], logf[:], 0.0, ALU.mult, ALU.add).then_inc(s.lsum_done, 1)
            dve.wait_ge(s.lsum_done, 1)
            v.scalar_tensor_tensor(out=u[:], in0=pv_bank[0][0:BH, 0:S], scalar=gbias[0:BH, :], in1=lsum[:],
                                   op0=ALU.add, op1=ALU.subtract).then_inc(s.u_done, 1)
            dve.wait_ge(s.u_done, 1)
            v.tensor_tensor_scan(cm[:], u[:], u[:], -3e38, ALU.max, ALU.max).then_inc(s.cm_done, 1)
            v.tensor_copy(parts[:, 0, :], u[:]).then_inc(s.hi_done, 1)
            dve.wait_ge(s.cm_done, 1)
            v.tensor_tensor(mld[:], cm[:], lsum[:], ALU.add).then_inc(s.mld_done, 1)
            v.tensor_scalar(nm[:], cm[:], -1.0, None, ALU.mult).then_inc(s.nm_done, 1)
            dve.wait_ge(s.nm_done, 1)
            v.tensor_copy(parts[:, 2, :], nm[:]).then_inc(s.hi_done, 1)
            dve.wait_ge(s.hi_done, 1)
            v.tensor_tensor(parts[:, 1, :], u[:], parts[:, 0, :].bitcast(F32), ALU.subtract).then_inc(s.parts_done, 1)
            dve.wait_ge(s.hi_done, 2)
            v.tensor_tensor(parts[:, 3, :], nm[:], parts[:, 2, :].bitcast(F32), ALU.subtract).then_inc(s.parts_done, 1)
            dve.wait_ge(s.iota_done, 5)

            def weigh(b):
                for half in range(2):
                    dve.wait_ge(s.dec_done, 2 * b + half + 1)
                    dve.wait_ge(s.qk_ps, b + 1)
                    if b >= 2:
                        dve.wait_ge(s.pv_ps, b - 1)
                    v.tensor_tensor(cw[:, b % 2, half * 4:half * 4 + 4, :],
                                    qk_bank(b, half)[:].rearrange("p (h t) -> p h t", t=S),
                                    dec[:, b % 2, half * 4:half * 4 + 4, :], ALU.mult).then_inc(s.cw_done, 1)

            def normalise(b):
                p = b % 2
                pv = pv_bank[b % 2][:, 0:NH * (DH + 1)].rearrange("p (h c) -> p h c", c=DH + 1)
                dve.wait_ge(s.pv_ps, b + 1)
                dve.wait_ge(s.emT_done, 1)
                v.tensor_tensor(den1[:, p, :], pv[:, :, DH], emT[:, NH * b:NH * b + NH], ALU.max).then_inc(s.den1_done, 1)
                dve.wait_ge(s.den1_done, b + 1)
                v.scalar_tensor_tensor(out=den[:, p, :], in0=pv[:, :, DH], scalar=-1.0, in1=den1[:, p, :],
                                       op0=ALU.mult, op1=ALU.max).then_inc(s.den_done, 1)
                dve.wait_ge(s.den_done, b + 1)
                v.tensor_scalar_add(den2[:, p, :], den[:, p, :], EPS_NORMALIZER).then_inc(s.den2_done, 1)
                dve.wait_ge(s.den2_done, b + 1)
                v.reciprocal(rden[:, p, :], den2[:, p, :]).then_inc(s.rden_done, 1)
                dve.wait_ge(s.rden_done, b + 1)
                v.tensor_tensor(hn[:, p, :].rearrange("p (h c) -> p h c", c=DH), pv[:, :, 0:DH],
                                rden[:, p, :].unsqueeze(2).to_broadcast([128, NH, DH]), ALU.mult).then_inc(s.hn_done, 1)
                dve.wait_ge(s.hn_done, b + 1)
                v.bn_stats(st2[:, p, :], hn[:, p, :]).then_inc(s.st2_done, 1)
                dve.wait_ge(s.st2_done, b + 1)
                v.bn_aggr(mv2[:, b, :], st2[:, p, :]).then_inc(s.mv2_done, 1)
                dve.wait_ge(s.mv2_done, b + 1)
                v.tensor_scalar_add(ve2[:, b:b + 1], mv2[:, b, 1:2], EPS_LN).then_inc(s.ve2_done, 1)

            def residual(b):
                p = b % 2
                v.scalar_tensor_tensor(out=hl[:, p, :], in0=hn[:, p, :], scalar=mv2[:, b, 0:1], in1=lnsb[:],
                                       op0=ALU.subtract, op1=ALU.mult).then_inc(s.hl_done, 1)
                dve.wait_ge(s.rs2_done, b + 1)
                dve.wait_ge(s.hl_done, b + 1)
                v.scalar_tensor_tensor(out=x2[:, b, :], in0=hl[:, p, :], scalar=rs2[:, b:b + 1], in1=xs[:, b, :],
                                       op0=ALU.mult, op1=ALU.add).then_inc(s.x2_done, 1)
                dve.wait_ge(s.x2_done, b + 1)
                v.bn_stats(st3[:, p, :], x2[:, b, :]).then_inc(s.st3_done, 1)
                dve.wait_ge(s.st3_done, b + 1)
                v.bn_aggr(mv3[:, b, :], st3[:, p, :]).then_inc(s.mv3_done, 1)
                dve.wait_ge(s.mv3_done, b + 1)
                v.tensor_scalar_add(ve3[:, b:b + 1], mv3[:, b, 1:2], EPS_LN).then_inc(s.ve3_done, 1)

            def norm2(b):
                dve.wait_ge(s.rs3_done, b + 1)
                v.tensor_scalar(xn[:, b, :], x2[:, b, :], mv3[:, b, 0:1], rs3[:, b:b + 1], ALU.subtract, ALU.mult)\
                    .then_inc(s.xn_done, 1)

            def choose(b):
                p = b % 2
                sc = misc[:, 400:408]
                dve.wait_ge(s.score_ps, b + 1)
                v.max(top[:, p, :], sc).then_inc(s.top_done, 1)
                dve.wait_ge(s.top_done, b + 1)
                v.max_index(topi[:, p, :], top[:, p, :], sc).then_inc(s.topi_done, 1)
                dve.wait_ge(s.topi_done, b + 1)
                v.tensor_copy(topf[:, p, :], topi[:, p, 0:2]).then_inc(s.topf_done, 1)
                dve.wait_ge(s.topf_done, b + 1)
                for k in range(2):
                    v.tensor_scalar(ohk[:, k, b, :], iota[:, 0:NE], topf[:, p, k:k + 1], None, ALU.is_equal)\
                        .then_inc(s.oh_done, 1)
                dve.wait_ge(s.oh_done, 2 * b + 2)
                v.tensor_tensor(maskb[:, b, :], ohk[:, 0, b, :], ohk[:, 1, b, :], ALU.add).then_inc(s.mask_done, 1)
                dve.wait_ge(s.mask_done, b + 1)
                v.tensor_tensor(prefb[:, b + 1, :], prefb[:, b, :], maskb[:, b, :], ALU.add).then_inc(s.pref_done, 1)
                dve.wait_ge(s.pref_done, b + 1)

            for i in range(B + 4):
                if i < B:
                    weigh(i)
                if 0 <= i - 1 < B:
                    normalise(i - 1)
                if 0 <= i - 2 < B:
                    residual(i - 2)
                if 0 <= i - 3 < B:
                    norm2(i - 3)
                if 0 <= i - 4 < B:
                    choose(i - 4)

            rk = bank[0][:, 0:BH]
            dve.wait_ge(s.rank_ps, 1)
            v.tensor_scalar(place[:], rk, float(MAIN), float(GAP), ALU.is_ge, ALU.mult).then_inc(s.ge_done, 1)
            dve.wait_ge(s.ge_done, 1)
            v.tensor_tensor(placed[:, 0, :, :], place[:].rearrange("p (b e) -> p b e", e=NE),
                            rk.rearrange("p (b e) -> p b e", e=NE), ALU.add).then_inc(s.place_done, 1)
            dve.wait_ge(s.place_done, 1)
            v.tensor_tensor(place[:].rearrange("p (b e) -> p b e", e=NE), placed[:, 0, :, :],
                            ebase[:].unsqueeze(1).to_broadcast([128, B, NE]), ALU.add).then_inc(s.base_done, 1)
            dve.wait_ge(s.base_done, 1)
            v.tensor_tensor(placed[:].rearrange("p k b e -> p k (b e)"), ohk[:].rearrange("p k b e -> p k (b e)"),
                            place[:].unsqueeze(1).to_broadcast([128, 2, BH]), ALU.mult).then_inc(s.placed_done, 1)
            dve.wait_ge(s.placed_done, 1)
            v.tensor_reduce(sl[:], placed[:].rearrange("p k b e -> p (k b) e"), axis=AX.X, op=ALU.add)\
                .then_inc(s.sl_done, 1)
            dve.wait_ge(s.sl_done, 1)
            v.tensor_copy(sli[:], sl[:]).then_inc(s.sli_done, 1)
            dve.wait_ge(s.sli_done, 1)
            v.tensor_scalar(ci[:], sli[:], 7, None, ALU.logical_shift_right).then_inc(s.split_done, 1)
            v.tensor_scalar(ri[:], sli[:], 127, None, ALU.bitwise_and).then_inc(s.split_done, 1)
            dve.wait_ge(s.split_done, 2)
            v.tensor_copy(cf[:], ci[:]).then_inc(s.splitf_done, 1)
            v.tensor_copy(rf[:], ri[:]).then_inc(s.splitf_done, 1)
            dve.wait_ge(s.splitf_done, 2)
            for b in range(B):
                for k in range(2):
                    j = k * B + b
                    v.tensor_scalar(ohb[:, j, :], iotab[:], rf[:, j:j + 1], None, ALU.is_equal).then_inc(s.oha_done, 1)
                    v.tensor_scalar(oha[:, j, :], iotab[:, 0:NC], cf[:, j:j + 1], tokval[:, b:b + 1],
                                    ALU.is_equal, ALU.mult).then_inc(s.oha_done, 1)
            v.tensor_reduce(cntf[:], bank[0][:, 128:128 + NE], axis=AX.X, op=ALU.max).then_inc(s.cnt_done, 1)
            dve.wait_ge(s.cnt_done, 1)
            v.tensor_copy(cnti[:], cntf[:]).then_inc(s.cnti_done, 1)
            lists = bank[1][:, 0:NC]
            dve.wait_ge(s.lists_ps, 1)
            v.scalar_tensor_tensor(out=padterm[:], in0=lists, scalar=0.0, in1=padval[:].rearrange("p a c -> p (a c)"),
                                   op0=ALU.is_equal, op1=ALU.mult).then_inc(s.padterm_done, 1)
            dve.wait_ge(s.padterm_done, 1)
            v.scalar_tensor_tensor(out=ids[:], in0=lists, scalar=float(2 * T), in1=padterm[:], op0=ALU.add, op1=ALU.add)\
                .then_inc(s.ids_done, 1)

            def split_x(e):
                dve.wait_ge(s.xT_ps, e + 1)
                if e >= 1:
                    dve.wait_ge(s.l1_ps, MC * e)
                v.tensor_copy(xhi[:], bank[5][:, 0:MAIN]).then_inc(s.xhi_done, 1)
                dve.wait_ge(s.xhi_done, e + 1)
                v.tensor_tensor(xlo[:], bank[5][:, 0:MAIN], xhi[:].bitcast(F32), ALU.subtract).then_inc(s.xlo_done, 1)

            def split_g(e, layer):
                gd, hd, ld, g, gh, gl = ((s.gelu1_done, s.g1h_done, s.g1l_done, g1, g1h, g1l),
                                         (s.gelu2_done, s.g2h_done, s.g2l_done, g2, g2h, g2l))[layer - 1]
                for m in range(MC):
                    dve.wait_ge(gd, MC * e + m + 1)
                    v.tensor_copy(gh[:, m, :], g[:, m, :]).then_inc(hd, 1)
                    dve.wait_ge(hd, MC * e + m + 1)
                    v.tensor_tensor(gl[:, m, :], g[:, m, :], gh[:, m, :].bitcast(F32), ALU.subtract).then_inc(ld, 1)

            def finish_y(e):
                dve.wait_ge(s.l3_ps, e + 1)
                v.tensor_scalar(yT[:], bank[4][:, 0:MAIN], smt[:, 64 + e:65 + e], 0.5, ALU.add, ALU.mult)\
                    .then_inc(s.yT_done, 1)

            def rows_y(e):
                dve.wait_ge(s.y_ps, e + 1)
                if e >= 2:
                    dve.wait_ge(s.added, 48 * (e - 1))
                v.tensor_copy(ys[:, e % 2, :, :], bank[6][:, 0:384].rearrange("p (c d) -> p c d", d=D)).then_inc(s.ys_done, 1)
            split_x(0)
            split_g(0, 1)
            for e in range(NE):
                if e + 1 < NE:
                    split_x(e + 1)
                if e >= 1:
                    rows_y(e - 1)
                split_g(e, 2)
                if e + 1 < NE:
                    split_g(e + 1, 1)
                finish_y(e)
                if e == 2:
                    most = most_tokens(dve)
            rows_y(NE - 1)

            with dve.If(most > MAIN):
                with dve.Fori(0, NE) as e:
                    for c in range(STEPS):
                        n = STEPS * e + c + 1
                        dve.wait_ge(s.r_turn, 3 * n - 2)
                        v.memset(turnd[:], 0.0)
                        v.tensor_copy(rbias[:, 0:MC], smt[:, bass.ds(MC * e, MC)])
                        v.tensor_copy(rbias[:, MC:2 * MC], smt[:, bass.ds(NE * MC + MC * e, MC)])
                        v.tensor_copy(rbias[:, 2 * MC:2 * MC + 1], smt[:, bass.ds(2 * NE * MC + e, 1)]).then_inc(s.r_bias, 1)
                        v.tensor_copy(rids[:], ids[:, bass.ds(CHUNKS * e + 3 + RC * c, RC)]).then_inc(s.r_ids, 1)
                        dve.wait_ge(s.r_xT, n)
                        v.tensor_copy(xhi[:, 0:REST], bank[5][:, 0:REST]).then_inc(s.r_xhi, 1)
                        dve.wait_ge(s.r_xhi, n)
                        v.tensor_tensor(xlo[:, 0:REST], bank[5][:, 0:REST], xhi[:, 0:REST].bitcast(F32), ALU.subtract)\
                            .then_inc(s.r_xlo, 1)
                        for gd, hd, ld, gt, gh, gl in ((s.r_gelu1, s.r_g1h, s.r_g1l, g1, g1h, g1l),
                                                       (s.r_gelu2, s.r_g2h, s.r_g2l, g2, g2h, g2l)):
                            dve.wait_ge(gd, MC * n)
                            v.tensor_copy(gh[:, :, 0:REST], gt[:, :, 0:REST]).then_inc(hd, 1)
                            dve.wait_ge(hd, n)
                            v.tensor_tensor(gl[:, :, 0:REST], gt[:, :, 0:REST], gh[:, :, 0:REST].bitcast(F32),
                                            ALU.subtract).then_inc(ld, 1)
                        dve.wait_ge(s.r_l3, n)
                        dve.wait_ge(s.r_bias, n)
                        v.tensor_scalar(yT[:, 0:REST], bank[4][:, 0:REST], rbias[:, 2 * MC:2 * MC + 1], 0.5,
                                        ALU.add, ALU.mult).then_inc(s.r_yT, 1)
                        dve.wait_ge(s.r_y, n)
                        v.tensor_copy(ys[:, 0, 0:RC, :], bank[6][:, 0:REST].rearrange("p (c d) -> p c d", d=D))\
                            .then_inc(s.r_ys, 1)

        @block.tensor
        def _(pe):
            t = nc.tensor
            pe.wait_ge(s.const_done, 1)
            pe.wait_ge(s.small_in, 16 * 27)
            t.transpose(bank[0][:, 0:128], sm[:], identf[:]).then_inc(s.sm_T, 1)
            for b in range(B):
                pe.wait_ge(ctx_in[b // 4], 16)
                t.transpose(bank[6 + b // 4][:, (b % 4) * S:(b % 4 + 1) * S], cs_in[:, b, :], identf[:]).then_inc(s.cT_ps, 1)
            for b in range(B):
                pe.wait_ge(s.qn_done, b + 1)
                t.transpose(arg_bank[b // 4][:, (b % 4) * S:(b % 4 + 1) * S], qn[:, b, :], identf[:]).then_inc(s.qT_ps, 1)
            pe.wait_ge(s.wpad_done, 4)
            pe.wait_ge(s.qT_done, 2)
            pe.wait_ge(s.cT_done, 2)
            for b in range(B):
                t.matmul(pv_bank[0][:, 0:S], wc[:, 2 * BH * b:2 * BH * (b + 1)], cT[:, b, :], start=(b == 0), stop=False)
                last = t.matmul(pv_bank[0][:, 0:S], wq[:, 2 * BH * b:2 * BH * (b + 1)], qT[:, b, :],
                                start=False, stop=(b == B - 1))
            last.then_inc(s.gates_ps, 1)

            def attend(b):
                pe.wait_ge(s.qbd_done, b + 1)
                if b == 0:
                    pe.wait_ge(s.smt_done, 1)
                for half in range(2):
                    if 2 * b + half >= 3:
                        pe.wait_ge(s.cw_done, 2 * b + half - 2)
                    last = t.matmul(qk_bank(b, half)[:], cT[:, b, :],
                                    qbd[:, b % 2, half * 4:half * 4 + 4, :].rearrange("p h t -> p (h t)"),
                                    start=True, stop=True)
                last.then_inc(s.qk_ps, 1)
                if b == 0:
                    pe.wait_ge(s.rows_in, 16 * 16)
                    pe.wait_ge(s.const_done, 7)
                pe.wait_ge(max_in[b % 2], 32 * (b // 2 + 1))
                for half in range(2):
                    if b >= 1:
                        pe.wait_ge(s.dec_done, 2 * b + half - 1)
                    dst = arg_bank[half][:].rearrange("p (h t) -> p h t", t=S)
                    t.matmul(dst, LT[:, b, :], RH[:, b % 2, 4 * half:4 * half + 4, :], start=True, stop=False)
                    t.matmul(dst, identb[:], negb[:].unsqueeze(1).to_broadcast([128, 4, S]), start=False, stop=True)\
                        .then_inc(s.arg_ps, 1)

            def values(b):
                if b >= 2:
                    pe.wait_ge(s.hn_done, b - 1)
                if b == 0:
                    pe.wait_ge(s.v1_done, 1)
                    pe.wait_ge(s.const_zero, 13)
                for h in range(NH):
                    pe.wait_ge(s.cw_done, 2 * b + h // 4 + 1)
                    last = t.matmul(pv_bank[b % 2][:, (DH + 1) * h:(DH + 1) * (h + 1)], cw[:, b % 2, h, :], v1[:, b, h, :],
                                    start=True, stop=True)
                last.then_inc(s.pv_ps, 1)

            def xn_transpose(b):
                pe.wait_ge(s.xn_done, b + 1)
                if b >= 1:
                    pe.wait_ge(s.topi_done, b)
                else:
                    pe.wait_ge(s.emT_done, 1)
                t.transpose(misc[:, 0:S], xn[:, b, :], identf[:]).then_inc(s.xnT_ps, 1)

            def scores(b):
                pe.wait_ge(s.xnT_done, b + 1)
                t.matmul(misc[:, 400:408], xnT[:, b % 2, :], smt[:, 72:80], start=True, stop=True)\
                    .then_inc(s.score_ps, 1)
            for i in range(B + 4):
                if i < B:
                    attend(i)
                if 0 <= i - 1 < B:
                    values(i - 1)
                if 0 <= i - 4 < B:
                    scores(i - 4)
                if 0 <= i - 3 < B:
                    xn_transpose(i - 3)
                if i == 0:
                    pe.wait_ge(s.em_done, 1)
                    t.transpose(misc[:, 0:BH], em[:], identf[0:BH, 0:BH]).then_inc(s.emT_ps, 1)
            pe.wait_ge(s.pref_done, B)
            t.matmul(bank[0][:, 0:BH], trib[:], maskb[:].rearrange("p b e -> p (b e)"), start=True, stop=False)
            t.matmul(bank[0][:, 0:BH], onesb[:], prefb[:, 0:B, :].rearrange("p b e -> p (b e)"), start=False, stop=True)
            t.matmul(bank[0][:, 128:128 + NE], onesb[:], prefb[:, B, :], start=True, stop=True).then_inc(s.rank_ps, 1)
            for i in range(2 * B):
                j = (i % 2) * B + i // 2
                pe.wait_ge(s.oha_done, 2 * (i + 1))
                last = t.matmul(bank[1][:, 0:NC], ohb[:, j, :], oha[:, j, :], start=(i == 0), stop=(i == 2 * B - 1))
            last.then_inc(s.lists_ps, 1)

            def x_transpose(e):
                pe.wait_ge(gathered[e % 2], 48 * (e // 2 + 1))
                if e >= 1:
                    pe.wait_ge(s.xlo_done, e)
                for c in range(3):
                    n = min(128, MAIN - 128 * c)
                    last = t.transpose(bank[5][:, 128 * c:128 * c + n], xg[0:n, e % 2, c, :], identf[0:n, 0:n])
                last.then_inc(s.xT_ps, 1)

            def product(dst, e, layer, m, ks, ahi, alo):
                p = e % 2
                n = 0
                for k in range(ks):
                    for w, act_ in ((whi, ahi), (wlo, ahi), (whi, alo)):
                        last = t.matmul(dst, wcol(w, p, layer, k, m), act_(k), start=(n == 0), stop=(n == 3 * ks - 1))
                        n += 1
                return last

            def layer1(e):
                pe.wait_ge(s.xlo_done, e + 1)
                pe.wait_ge(s.wlo_done, e + 1)
                for m in range(MC):
                    if e >= 1:
                        pe.wait_ge(s.gelu2_done, MC * (e - 1) + m + 1)
                    product(bank[m][:, 0:MAIN], e, 1, m, 1, lambda k: xhi[:], lambda k: xlo[:]).then_inc(s.l1_ps, 1)

            def layer2(e):
                pe.wait_ge(s.g1l_done, MC * (e + 1))
                for m in range(MC):
                    product(bank[m][:, 0:MAIN], e, 2, m, MC, lambda k: g1h[:, k, :], lambda k: g1l[:, k, :])\
                        .then_inc(s.l2_ps, 1)
                    if m == 0 and e + 1 < NE:
                        x_transpose(e + 1)
                    if m == 1 and e >= 1:
                        y_transpose(e - 1)

            def layer3(e):
                pe.wait_ge(s.g2l_done, MC * (e + 1))
                if e >= 1:
                    pe.wait_ge(s.yT_done, e)
                product(bank[4][:, 0:MAIN], e, 3, 0, MC, lambda k: g2h[:, k, :], lambda k: g2l[:, k, :])\
                    .then_inc(s.l3_ps, 1)

            def y_transpose(e):
                pe.wait_ge(s.yT_done, e + 1)
                if e >= 1:
                    pe.wait_ge(s.ys_done, e)
                for c in range(3):
                    n = min(128, MAIN - 128 * c)
                    last = t.transpose(bank[6][0:n, 128 * c:128 * c + D], yT[:, 128 * c:128 * c + n], identf[:])
                last.then_inc(s.y_ps, 1)
            x_transpose(0)
            layer1(0)
            for e in range(NE):
                layer2(e)
                if e + 1 < NE:
                    layer1(e + 1)
                layer3(e)
                if e == 2:
                    most = most_tokens(pe)
            y_transpose(NE - 1)

            with pe.If(most > MAIN):
                with pe.Fori(0, NE) as e:
                    for c in range(STEPS):
                        n = STEPS * e + c + 1
                        pe.wait_ge(s.r_gathered, 16 * RC * n)
                        for j in range(RC):
                            last = t.transpose(bank[5][:, 128 * j:128 * j + 128], xg[:, 0, j, :], identf[:])
                        last.then_inc(s.r_xT, 1)
                        pe.wait_ge(s.r_xlo, n)
                        if c == 0:
                            pe.wait_ge(s.r_wlo, e + 1)
                        for m in range(MC):
                            last = product(bank[m][:, 0:REST], 0, 1, m, 1, lambda k: xhi[:, 0:REST], lambda k: xlo[:, 0:REST])
                        last.then_inc(s.r_l1, 1)
                        pe.wait_ge(s.r_g1l, n)
                        for m in range(MC):
                            last = product(bank[m][:, 0:REST], 0, 2, m, MC, lambda k: g1h[:, k, 0:REST],
                                           lambda k: g1l[:, k, 0:REST])
                        last.then_inc(s.r_l2, 1)
                        pe.wait_ge(s.r_g2l, n)
                        product(bank[4][:, 0:REST], 0, 3, 0, MC, lambda k: g2h[:, k, 0:REST],
                                lambda k: g2l[:, k, 0:REST]).then_inc(s.r_l3, 1)
                        pe.wait_ge(s.r_yT, n)
                        for j in range(RC):
                            last = t.transpose(bank[6][:, 128 * j:128 * j + D], yT[:, 128 * j:128 * j + 128], identf[:])
                        last.then_inc(s.r_y, 1)


NAMES = ["x", "ctx_1024", "L0_xattn_igate_w", "L0_xattn_igate_b", "L0_xattn_fgate_w", "L0_xattn_fgate_b",
         "L0_xattn_ln_scale", "L0_ffn_expert_tokens", "L0_ffn_W1", "L0_ffn_b1", "L0_ffn_W2", "L0_ffn_b2",
         "L0_ffn_W3", "L0_ffn_b3"]


def kernel(**inputs):
    import numpy as _np
    import concourse.bacc as _bacc
    from concourse import mybir as _mybir
    from concourse.bass_utils import run_bass_kernel_spmd as _run

    nc = _bacc.Bacc("TRN2", target_bir_lowering=False, num_devices=1)
    arrays, args = {}, []
    for name in NAMES:
        a = _np.ascontiguousarray(inputs[name])
        arrays[f"in_{name}"] = a
        args.append(nc.dram_tensor(f"in_{name}", a.shape, _mybir.dt.from_np(a.dtype), kind="ExternalInput").ap())
    out = nc.dram_tensor("out_rows", (T + PAD, D), F32, kind="ExternalOutput").ap()
    build(nc, *args, out)
    r = _run(nc, [arrays], core_ids=[0])
    return r.results[0]["out_rows"][0:T].reshape(B, S, D)
```

```python
from collections import namedtuple
from contextlib import ExitStack

import numpy as np
import concourse.bass as bass
from concourse import mybir

F32 = mybir.dt.float32
F32R = mybir.dt.float32r
BF16 = mybir.dt.bfloat16
F16 = mybir.dt.float16
I32 = mybir.dt.int32
U32 = mybir.dt.uint32
ALU = mybir.AluOpType
ACT = mybir.ActivationFunctionType
AX = mybir.AxisListType

B, S, D = 8, 128, 128
NH = 8
DH = D // NH
BH = B * NH
NE = 8
HID = 512
MC = HID // 128
T = B * S
EPS_NORMALIZER = 1e-6
EPS_LN = 1e-5
NEG = -1e38

MAIN = 320
CHUNKS = 9
GAP = 3 * 128 - MAIN
PLACES = CHUNKS * 128
RC = 2
REST = RC * 128
PAD = 3 * 128
ROUND = 1.5 * 2.0 ** 23
NC = NE * CHUNKS
STEPS = (CHUNKS - 3) // RC
WCOLS = HID + MC * HID + MC * D


def build(nc, x, ctx, igw, igb, fgw, fgb, lns, et, W1, b1, W2, b2, W3, b3, out):
    es = ExitStack()
    with es:
        def sb(name, shape, dt=F32):
            return es.enter_context(nc.sbuf_tensor(name, shape, dt))

        def sem(name):
            return es.enter_context(nc.semaphore(name))

        xnd = nc.dram_tensor("xn_rows", (T + PAD, D), F32, kind="Internal").ap()

        wraw = sb("wraw", [128, NE, WCOLS])
        whi = [sb("whi0", [128, WCOLS], F32R)]
        wlo = [sb("wlo0", [128, WCOLS], F32R)]
        identf = sb("identf", [128, 128])
        identb = sb("identb", [128, 128], BF16)
        negb = sb("negb", [128, 128], BF16)
        trib = sb("trib", [128, 128], BF16)
        onesb = sb("onesb", [128, 128], BF16)
        iota = sb("iota", [128, 128])
        iotab = sb("iotab", [128, 128], F16)
        hmask = sb("hmask", [128, NH])
        minus_half = sb("minus_half", [128, NH])
        tokval = sb("tokval", [128, B])
        padval = sb("padval", [128, NC // 3, 3])
        ebase = sb("ebase", [128, NE])
        zrow = sb("zrow", [128, D])
        ones64 = sb("ones64", [BH, S])
        onecol = sb("onecol", [128, 1])
        sm = sb("sm", [128, 128])
        smt = sb("smt", [128, 128])
        gbias = sb("gbias", [128, 1])
        lnsb = sb("lnsb", [128, D])
        b3h = sb("b3h", [128, NE])
        ohk = sb("ohk", [128, B, 2, NE])
        maskb = sb("maskb", [128, B, NE], BF16)
        prefb = sb("prefb", [128, B + 1, NE], BF16)
        top = sb("top", [128, B, 8])
        topi = sb("topi", [128, B, 8], U32)
        topf = sb("topf", [128, B, 2])
        beyond = sb("beyond", [128, 2, NE])
        place = sb("place", [128, 2, NE])
        placed = sb("placed", [128, 2, 2, NE])
        sl = sb("sl", [128, B, 2])
        slf = sb("slf", [128, B, 2])
        cf = sb("cf", [128, B, 2])
        rf = sb("rf", [128, B, 2])
        padterm = sb("padterm", [128, NC])
        ids = sb("ids", [128, NC], U32)
        cntf = sb("cntf", [128, 1])
        cnti = sb("cnti", [128, 1], I32)
        rids = sb("rids", [128, RC], U32)
        rbias = sb("rbias", [128, 2 * MC + 1])
        turn = sb("turn", [128, 1])
        turnd = sb("turnd", [128, 1])

        attn = ExitStack()

        def at(name, shape, dt=F32):
            return attn.enter_context(nc.sbuf_tensor(name, shape, dt))

        xs = at("xs", [128, B, D])
        cs_in = at("cs_in", [128, B, D])
        qn = at("qn", [128, B, D])
        qT = at("qT", [128, B, S])
        cT = at("cT", [128, B, S])
        v1 = at("v1", [128, B, NH, DH + 1])
        st1 = at("st1", [128, B, 6])
        mv1 = at("mv1", [128, B, 2])
        ve1 = at("ve1", [128, B])
        rs1 = at("rs1", [128, B])
        emT = at("emT", [128, BH])
        emTe = at("emTe", [128, BH])
        em = at("em", [BH, S])
        um = at("um", [128, S])
        parts = at("parts", [128, 3, S], BF16)
        LT = at("LT", [3 * NH + 3, B, S], BF16)
        RH = at("RH", [3 * NH + 3, BH, S], BF16)
        delta = at("delta", [3 * NH, NH])
        qbd = at("qbd", [128, 2, NH, S])
        dec = at("dec", [128, 2, NH, S])
        cw = dec
        den1 = at("den1", [128, 2, 2, NH])
        den2 = at("den2", [128, 2, 2, NH])
        den = at("den", [128, 2, 2, NH])
        rden = at("rden", [128, 2, 2, NH])
        gates = ExitStack()

        def gt(name, shape, dt=F32):
            return gates.enter_context(nc.sbuf_tensor(name, shape, dt))
        fgt = gt("fgt", [BH, S])
        nabs = gt("nabs", [BH, S])
        expn = gt("expn", [BH, S])
        logf = gt("logf", [BH, S])
        lsum = gt("lsum", [BH, S])
        cm = gt("cm", [BH, S])
        mld = gt("mld", [BH, S])
        um1 = gt("um1", [128, S])
        gates.close()
        hn = at("hn", [128, 2, 2, D])
        hl = at("hl", [128, 2, 2, D])
        st2 = at("st2", [128, 2, 2, 6])
        mv2 = at("mv2", [128, B, 2])
        ve2 = at("ve2", [128, B])
        rs2 = at("rs2", [128, B])
        x2 = at("x2", [128, B, D])
        st3 = at("st3", [128, 2, 2, 6])
        mv3 = at("mv3", [128, B, 2])
        ve3 = at("ve3", [128, B])
        rs3 = at("rs3", [128, B])
        xn = qn
        xnT = at("xnT", [128, 2, S])
        mark = ExitStack()
        wq = mark.enter_context(nc.sbuf_tensor("wq", [128, B * (BH * 2 + NH)], F32))
        wc = mark.enter_context(nc.sbuf_tensor("wc", [128, B * (BH * 2 + NH)], F32))
        mark.close()
        ohb = at("ohb", [128, 2 * B, 128], F16)
        oha = at("oha", [128, 2 * B, NC], F16)
        attn.close()
        whi.append(sb("whi1", [128, WCOLS], F32R))
        wlo.append(sb("wlo1", [128, WCOLS], F32R))
        xg = sb("xg", [128, 2, 3, D])
        xhi = sb("xhi", [128, MAIN], F32R)
        xlo = sb("xlo", [128, MAIN], F32R)
        g1 = sb("g1", [128, MC, MAIN])
        g1h = sb("g1h", [128, MC, MAIN], F32R)
        g1l = sb("g1l", [128, MC, MAIN], F32R)
        g2 = sb("g2", [128, MC, MAIN])
        g2h = sb("g2h", [128, MC, MAIN], F32R)
        g2l = sb("g2l", [128, MC, MAIN], F32R)
        yT = sb("yT", [128, MAIN])
        ys = sb("ys", [128, 2, 3, D])

        bank = [es.enter_context(nc.psum_tensor(f"bank{i}", [128, 512], F32)) for i in range(8)]

        names = """
        x_in0 x_in1 ctx_in0 ctx_in1 small_in bias_in w_in0 w_in1 w_in2 w_in3 w_in4 w_in5 w_in6 w_in7
        const_zero const_done const2_done iota_done ve1_done rs1_done st1_done mv1_done qn_done sm_T smt_done b3h_done
        qT_ps cT_ps qT_done cT_done wq_zero wpad_done v1_done gates_ps
        fgt_done nabs_done expn_done softplus_done logf_done lsum_done u_done cm_done mld_done um_done em_done
        um1_done part_done rows_in emT_ps max_in emT_done delta_done rh_done lt_ones
        qbd_done qk_ps arg_ps dec_done cw_done pv_ps den1_done den2_done den_done rden_done hn_done st2_done mv2_done
        ve2_done rs2_done hl_done x2_done st3_done mv3_done ve3_done rs3_done xn_done xnT_ps xnT_done score_ps
        top_done topi_done topf_done oh_done mask_done pref_done rank_ps beyond_done place_done base_done placed_done
        sl_done slf_done cf_done rf_done oha_done lists_ps padterm_done ids_done cnt_done cnti_done
        xn_out x2_out gathered0 gathered1 whi_done wlo_done wlo13_done xT_ps xhi_done xlo_done l1_ps gelu1_done g1h_done
        g1l_done l2_ps gelu2_done g2h_done g2l_done l3_ps yT_done y_ps ys_done added
        r_turn r_whi r_wlo r_ids r_bias r_gathered r_xT r_xhi r_xlo r_l1 r_gelu1 r_g1h r_g1l
        r_l2 r_gelu2 r_g2h r_g2l r_l3 r_yT r_y r_ys r_added
        """.split()
        s = namedtuple("Semaphores", names)(*[sem(n) for n in names])
        x_in = [s.x_in0, s.x_in1]
        ctx_in = [s.ctx_in0, s.ctx_in1]
        gathered = [s.gathered0, s.gathered1]
        w_in = [s.w_in0, s.w_in1, s.w_in2, s.w_in3, s.w_in4, s.w_in5, s.w_in6, s.w_in7]

        def wcol(w, p, layer, k, m):
            at_ = {1: 0, 2: HID, 3: HID + MC * HID}[layer]
            width = D if layer == 3 else HID
            c = at_ + k * width + m * 128
            return w[p][:, c:c + 128]

        def most_tokens(engine):
            engine.wait_ge(s.cnti_done, 1)
            return engine.value_load(cnti[0:1, 0:1], min_val=0, max_val=T)

        def qk_bank(b, half):
            return bank[(2 * b + half) % 3]

        arg_bank = bank[3:5]
        pv_bank = bank[5:7]
        misc = bank[7]
        lists_bank = bank[0]

        block = es.enter_context(nc.Block())

        @block.sync
        def _(sp):
            half = B // 2
            for i in range(2):
                sp.dma_start(xs[:, i * half:(i + 1) * half, :],
                             x[i * half:(i + 1) * half].rearrange("b s d -> s b d")).then_inc(x_in[i], 16)
                sp.dma_start(cs_in[:, i * half:(i + 1) * half, :],
                             ctx[i * half:(i + 1) * half].rearrange("b s d -> s b d")).then_inc(ctx_in[i], 16)
            for e in range(NE):
                sp.dma_start(wraw[:, e, 0:HID], W1[e]).then_inc(w_in[e], 16)
                sp.dma_start(wraw[:, e, HID:HID + MC * HID].rearrange("p (k n) -> p k n", k=MC),
                             W2[e].rearrange("(k p) n -> p k n", p=128)).then_inc(w_in[e], 16)
                sp.dma_start(wraw[:, e, HID + MC * HID:].rearrange("p (k n) -> p k n", k=MC),
                             W3[e].rearrange("(k p) n -> p k n", p=128)).then_inc(w_in[e], 16)

            sp.wait_ge(s.const_zero, 13)
            zeros = zrow[:].unsqueeze(1).to_broadcast([128, PAD // 128, D])
            sp.dma_start(xnd[T:T + PAD, :].rearrange("(c p) d -> p c d", p=128), zeros).then_inc(s.xn_out, 16)
            sp.dma_start(out[T:T + PAD, :].rearrange("(c p) d -> p c d", p=128), zeros).then_inc(s.x2_out, 16)
            for b in range(B):
                sp.wait_ge(s.x2_done, b + 1)
                sp.dma_start(out[b * S:(b + 1) * S, :], x2[:, b, :]).then_inc(s.x2_out, 16)
                sp.wait_ge(s.xn_done, b + 1)
                sp.dma_start(xnd[b * S:(b + 1) * S, :], xn[:, b, :]).then_inc(s.xn_out, 16)

        @block.gpsimd
        def _(pool):
            g = nc.gpsimd
            g.memset(wq[:], 0.0).then_inc(s.wq_zero, 1)
            g.memset(wc[:], 0.0).then_inc(s.wq_zero, 1)
            g.memset(identf[:], 0.0).then_inc(s.const_zero, 1)
            g.memset(hmask[:], 0.25).then_inc(s.const_zero, 1)
            g.memset(minus_half[:], -0.5).then_inc(s.const_zero, 1)
            g.memset(identb[:], 0.0).then_inc(s.const_zero, 1)
            g.memset(negb[:], NEG).then_inc(s.const_zero, 1)
            g.memset(trib[:], 1.0).then_inc(s.const_zero, 1)
            g.memset(onesb[:], 1.0).then_inc(s.const_zero, 1)
            g.memset(delta[:], 1.0).then_inc(s.const_zero, 1)
            g.memset(zrow[:], 0.0).then_inc(s.const_zero, 1)
            g.memset(ones64[:], 1.0).then_inc(s.const_zero, 1)
            g.memset(onecol[:], 1.0).then_inc(s.const_zero, 1)
            g.memset(prefb[:, 0, :], 0.0).then_inc(s.const_zero, 1)
            g.memset(v1[:, :, :, DH:DH + 1], 1.0).then_inc(s.const_zero, 1)
            g.memset(LT[:], 1.0).then_inc(s.lt_ones, 1)
            pool.wait_ge(s.const_zero, 13)
            g.affine_select(out=identf[:], in_=identf[:], compare_op=ALU.not_equal, fill=1.0, base=0,
                            pattern=[[-1, 128]], channel_multiplier=1).then_inc(s.const_done, 1)
            g.affine_select(out=identb[:], in_=identb[:], compare_op=ALU.not_equal, fill=1.0, base=0,
                            pattern=[[-1, 128]], channel_multiplier=1).then_inc(s.const_done, 1)
            g.affine_select(out=negb[:], in_=negb[:], compare_op=ALU.is_gt, fill=0.0, base=0,
                            pattern=[[-1, 128]], channel_multiplier=1).then_inc(s.const_done, 1)
            g.affine_select(out=trib[:], in_=trib[:], compare_op=ALU.is_gt, fill=0.0, base=0,
                            pattern=[[1, 128]], channel_multiplier=-1).then_inc(s.const_done, 1)
            g.affine_select(out=hmask[:], in_=hmask[:], compare_op=ALU.is_ge, fill=0.0, base=0,
                            pattern=[[-DH, NH]], channel_multiplier=1).then_inc(s.const_done, 1)
            pool.wait_ge(s.const_done, 5)
            g.affine_select(out=hmask[:], in_=hmask[:], compare_op=ALU.is_ge, fill=0.0, base=DH - 1,
                            pattern=[[DH, NH]], channel_multiplier=-1).then_inc(s.const_done, 1)
            g.affine_select(out=delta[:], in_=delta[:], compare_op=ALU.is_ge, fill=0.0, base=0,
                            pattern=[[-3, NH]], channel_multiplier=1).then_inc(s.const_done, 1)
            pool.wait_ge(s.const_done, 7)
            g.affine_select(out=delta[:], in_=delta[:], compare_op=ALU.is_ge, fill=0.0, base=2,
                            pattern=[[3, NH]], channel_multiplier=-1).then_inc(s.delta_done, 1)
            g.iota(iota[:], pattern=[[1, 128]], base=0, channel_multiplier=0,
                   allow_small_or_imprecise_dtypes=True).then_inc(s.iota_done, 1)
            g.iota(iotab[:], pattern=[[1, 128]], base=0, channel_multiplier=0,
                   allow_small_or_imprecise_dtypes=True).then_inc(s.iota_done, 1)
            g.iota(tokval[:], pattern=[[S, B]], base=-2 * T, channel_multiplier=1,
                   allow_small_or_imprecise_dtypes=True).then_inc(s.iota_done, 1)
            g.iota(padval[:], pattern=[[0, NC // 3], [128, 3]], base=-T, channel_multiplier=1,
                   allow_small_or_imprecise_dtypes=True).then_inc(s.iota_done, 1)
            g.iota(ebase[:], pattern=[[PLACES, NE]], base=0, channel_multiplier=0,
                   allow_small_or_imprecise_dtypes=True).then_inc(s.iota_done, 1)
            pool.wait_ge(ctx_in[0], 16)
            pool.wait_ge(ctx_in[1], 16)
            g.tensor_copy(v1[:, :, :, 0:DH], cs_in[:].rearrange("p b (h c) -> p b h c", c=DH)).then_inc(s.v1_done, 1)
            pool.wait_ge(s.ve1_done, 1)
            g.tensor_tensor(rs1[:], ve1[:], minus_half[:], ALU.pow).then_inc(s.rs1_done, 1)

            def make_qbd(b):
                if b >= 2:
                    pool.wait_ge(s.qk_ps, 2 * (b - 1))
                g.tensor_tensor(qbd[:, b % 2, :, :], qT[:, b:b + 1, :].to_broadcast([128, NH, S]),
                                hmask[:].unsqueeze(2).to_broadcast([128, NH, S]), ALU.mult).then_inc(s.qbd_done, 1)
            pool.wait_ge(s.qT_done, 2)
            make_qbd(0)
            make_qbd(1)

            def rsqrt(dst, src, wait, done, j):
                pool.wait_ge(wait, j + 1)
                g.tensor_tensor(dst[:, 2 * j:2 * j + 2], src[:, 2 * j:2 * j + 2], minus_half[:, 0:2], ALU.pow)\
                    .then_inc(done, 1)
            for j in range(B // 2 + 1):
                if j + 1 < B // 2:
                    make_qbd(2 * j + 2)
                if j >= 1:
                    rsqrt(rs2, ve2, s.ve2_done, s.rs2_done, j - 1)
                if j + 1 < B // 2:
                    make_qbd(2 * j + 3)
                if j >= 1:
                    rsqrt(rs3, ve3, s.ve3_done, s.rs3_done, j - 1)

            def gather(e):
                if e >= 2:
                    pool.wait_ge(s.xT_ps, e - 1)
                for c in range(3):
                    n = min(128, MAIN - 128 * c)
                    col = CHUNKS * e + c
                    g.indirect_dma_start(out=xg[0:n, e % 2, c, :], out_offset=None, in_=xnd,
                                         in_offset=bass.IndirectOffsetOnAxis(ap=ids[0:n, col:col + 1], axis=0))\
                        .then_inc(gathered[e % 2], 16)

            def weights_lo(e):
                pool.wait_ge(s.whi_done, e + 1)
                for a_, b_ in ((0, HID), (HID + MC * HID, WCOLS)):
                    g.tensor_tensor(wlo[e % 2][:, a_:b_], wraw[:, e, a_:b_], whi[e % 2][:, a_:b_].bitcast(F32),
                                    ALU.subtract).then_inc(s.wlo13_done, 1)

            def scatter(e):
                pool.wait_ge(s.ys_done, e + 1)
                if e >= 1:
                    pool.wait_ge(s.added, 48 * e)
                for c in range(3):
                    n = min(128, MAIN - 128 * c)
                    col = CHUNKS * e + c
                    g.indirect_dma_start(out=out, out_offset=bass.IndirectOffsetOnAxis(ap=ids[0:n, col:col + 1], axis=0),
                                         in_=ys[0:n, e % 2, c, :], in_offset=None, compute_op=ALU.add)\
                        .then_inc(s.added, 16)
            weights_lo(0)
            pool.wait_ge(s.ids_done, 1)
            pool.wait_ge(s.xn_out, 16 * (B + 1))
            pool.wait_ge(s.x2_out, 16 * (B + 1))
            gather(0)
            gather(1)
            weights_lo(1)
            for e in range(NE):
                if e >= 1 and e + 1 < NE:
                    gather(e + 1)
                    weights_lo(e + 1)
                if e >= 1:
                    scatter(e - 1)
                if e == 2:
                    most = most_tokens(pool)
            scatter(NE - 1)
            pool.wait_ge(s.added, 48 * NE)

            def tick(before=None):
                if before is not None:
                    pool.wait_ge(s.r_turn, before)
                g.tensor_tensor(turn[:], onecol[:], onecol[:], ALU.mult).then_inc(s.r_turn, 1)

            with pool.If(most > MAIN):
                tick()
                with pool.Fori(0, NE) as e:
                    pool.wait_ge(s.r_whi, e + 1)
                    g.tensor_tensor(wlo[0][:], wraw[:, bass.ds(e, 1), :].rearrange("p o w -> p (o w)"),
                                    whi[0][:].bitcast(F32), ALU.subtract).then_inc(s.r_wlo, 1)
                    for c in range(STEPS):
                        over = STEPS * e + c
                        pool.wait_ge(s.r_ids, over + 1)
                        tick(3 * over + 1)
                        for j in range(RC):
                            g.indirect_dma_start(out=xg[:, 0, j, :], out_offset=None, in_=xnd,
                                                 in_offset=bass.IndirectOffsetOnAxis(ap=rids[:, j:j + 1], axis=0))\
                                .then_inc(s.r_gathered, 16)
                        pool.wait_ge(s.r_ys, over + 1)
                        tick(3 * over + 2)
                        for j in range(RC):
                            g.indirect_dma_start(out=out, out_offset=bass.IndirectOffsetOnAxis(ap=rids[:, j:j + 1], axis=0),
                                                 in_=ys[:, 0, j, :], in_offset=None, compute_op=ALU.add)\
                                .then_inc(s.r_added, 16)
                        pool.wait_ge(s.r_added, 16 * RC * (over + 1))
                        tick(3 * over + 3)

        @block.scalar
        def _(act):
            a = nc.scalar
            a.preload_act_table_set("natural_log_exp_and_others")
            for c in range(3):
                act.dma_start(sm[80 + 8 * c:88 + 8 * c, :], igw[:, c * D:(c + 1) * D]).then_inc(s.small_in, 16)
                act.dma_start(sm[104 + 8 * c:112 + 8 * c, :], fgw[:, c * D:(c + 1) * D]).then_inc(s.small_in, 16)
            for lo, rows, src in ((0, NE * MC, b1.rearrange("e (m p) -> (e m) p", p=128)),
                                  (32, NE * MC, b2.rearrange("e (m p) -> (e m) p", p=128)),
                                  (64, NE, b3), (72, NE, et)):
                act.dma_start(sm[lo:lo + rows, :], src).then_inc(s.small_in, 16)
            for lo, src in ((0, igb), (BH, fgb)):
                act.dma_start(gbias[lo:lo + BH, :], src.rearrange("(o h) -> o h", o=1).to_broadcast([B, NH]))\
                    .then_inc(s.bias_in, 16)
            act.dma_start(lnsb[:], lns.partition_broadcast(128)).then_inc(s.bias_in, 16)
            act.wait_ge(s.delta_done, 1)
            a.activation(RH[0:3 * NH, :, :].rearrange("p (b h) t -> p b h t", h=NH),
                         delta[:].unsqueeze(1).unsqueeze(3).to_broadcast([3 * NH, B, NH, S]), ACT.Copy)\
                .then_inc(s.rh_done, 1)
            act.wait_ge(s.qT_ps, 4)
            a.activation(qT[:, 0:4, :], arg_bank[0][:].rearrange("p (b t) -> p b t", t=S), ACT.Copy).then_inc(s.qT_done, 1)
            act.wait_ge(s.qT_ps, 8)
            a.activation(qT[:, 4:8, :], arg_bank[1][:].rearrange("p (b t) -> p b t", t=S), ACT.Copy).then_inc(s.qT_done, 1)
            act.wait_ge(s.nabs_done, 1)
            a.activation(expn[:], nabs[:], ACT.Exp).then_inc(s.expn_done, 1)
            act.wait_ge(s.expn_done, 1)
            a.activation(nabs[:], expn[:], ACT.Ln, bias=onecol[0:BH, :]).then_inc(s.softplus_done, 1)
            act.wait_ge(s.mld_done, 1)
            a.activation(em[:], mld[:], ACT.Exp, scale=-1.0).then_inc(s.em_done, 1)
            act.wait_ge(s.part_done, 3)
            act.wait_ge(s.lt_ones, 1)
            for q in range(3):
                act.dma_start(RH[3 * NH + q:3 * NH + q + 1, :, :], parts[BH:128, q, :]).then_inc(s.max_in, 16)
            for b in range(B):
                act.dma_start(LT[0:3 * NH, b, :], parts[NH * b:NH * b + NH, :, :]).then_inc(s.max_in, 16)
            act.wait_ge(s.emT_ps, 1)
            a.activation(emT[:], misc[:, 0:BH], ACT.Copy).then_inc(s.emT_done, 1)

            def decay(b):
                if b >= 2:
                    act.wait_ge(s.pv_ps, b - 1)
                for half in range(2):
                    act.wait_ge(s.arg_ps, 2 * b + half + 1)
                    a.activation(dec[:, b % 2, half * 4:half * 4 + 4, :],
                                 arg_bank[half][:].rearrange("p (h t) -> p h t", t=S), ACT.Exp).then_inc(s.dec_done, 1)
            for j in range(B // 2 + 2):
                if j < B // 2:
                    decay(2 * j)
                if j >= 2:
                    act.wait_ge(s.xnT_ps, j - 1)
                    a.activation(xnT[:], misc[:, 0:2 * S].rearrange("p (i t) -> p i t", t=S), ACT.Copy)\
                        .then_inc(s.xnT_done, 1)
                if j < B // 2:
                    decay(2 * j + 1)
            a.preload_act_table(ACT.Gelu)

            def weights_hi(e):
                act.wait_ge(w_in[e], 48)
                if e >= 2:
                    act.wait_ge(s.l3_ps, e - 1)
                a.activation(whi[e % 2][:], wraw[:, e, :], ACT.Copy).then_inc(s.whi_done, 1)

            def gelu(e, layer):
                psd, done, split, dst, col = ((s.l1_ps, s.gelu1_done, s.g1l_done, g1, 0),
                                              (s.l2_ps, s.gelu2_done, s.g2l_done, g2, 32))[layer - 1]
                for m in range(MC):
                    act.wait_ge(psd, MC * e + m + 1)
                    if e >= 1:
                        act.wait_ge(split, MC * (e - 1) + m + 1)
                    a.activation(dst[:, m, :], bank[m][:, 0:MAIN], ACT.Gelu,
                                 bias=smt[:, col + MC * e + m:col + MC * e + m + 1]).then_inc(done, 1)
            def scale_y(e):
                act.wait_ge(s.l3_ps, e + 1)
                if e >= 1:
                    act.wait_ge(s.y_ps, e)
                a.activation(yT[:], bank[4][:, 0:MAIN], ACT.Identity, bias=b3h[:, e:e + 1], scale=0.5)\
                    .then_inc(s.yT_done, 1)
            weights_hi(0)
            act.wait_ge(s.ids_done, 1)
            act.wait_ge(s.xn_out, 16 * (B + 1))
            act.wait_ge(s.x2_out, 16 * (B + 1))
            weights_hi(1)
            gelu(0, 1)
            for e in range(NE):
                if 1 <= e and e + 1 < NE:
                    weights_hi(e + 1)
                gelu(e, 2)
                if e + 1 < NE:
                    gelu(e + 1, 1)
                scale_y(e)
                if e == 2:
                    most = most_tokens(act)

            with act.If(most > MAIN):
                with act.Fori(0, NE) as e:
                    act.wait_ge(s.r_turn, 3 * STEPS * e + 1)
                    a.activation(whi[0][:], wraw[:, bass.ds(e, 1), :].rearrange("p o w -> p (o w)"), ACT.Copy)\
                        .then_inc(s.r_whi, 1)
                    for c in range(STEPS):
                        for psd, done, dst, col in ((s.r_l1, s.r_gelu1, g1, 0), (s.r_l2, s.r_gelu2, g2, MC)):
                            act.wait_ge(psd, STEPS * e + c + 1)
                            for m in range(MC):
                                a.activation(dst[:, m, 0:REST], bank[m][:, 0:REST], ACT.Gelu,
                                             bias=rbias[:, col + m:col + m + 1]).then_inc(done, 1)

        @block.vector
        def _(dve):
            v = nc.vector
            for b in range(B):
                dve.wait_ge(x_in[b // 4], 16)
                v.bn_stats(st1[:, b, :], xs[:, b, :]).then_inc(s.st1_done, 1)
            for b in range(B):
                dve.wait_ge(s.st1_done, b + 1)
                v.bn_aggr(mv1[:, b, :], st1[:, b, :]).then_inc(s.mv1_done, 1)
            dve.wait_ge(s.mv1_done, B)
            v.tensor_scalar_add(ve1[:], mv1[:, :, 1], EPS_LN).then_inc(s.ve1_done, 1)
            dve.wait_ge(s.sm_T, 1)
            v.tensor_copy(smt[:], bank[0][:, 0:128]).then_inc(s.smt_done, 1)
            dve.wait_ge(s.smt_done, 1)
            v.tensor_scalar(b3h[:], smt[:, 64:72], 0.5, None, ALU.mult).then_inc(s.b3h_done, 1)
            dve.wait_ge(s.wq_zero, 2)
            pad = BH * 2 + NH

            def padded(w):
                return w[:].rearrange("p (b c) -> p b c", c=pad)[:, :, 0:2 * BH]\
                    .rearrange("p b (g c) -> p b g c", c=BH)[:, :, :, 0:NH]

            def gate_part(c):
                return smt[:, 80:128].rearrange("p (g c h) -> p g c h", g=2, c=3)[:, :, c, :]\
                    .unsqueeze(1).to_broadcast([128, B, 2, NH])
            for gg in range(2):
                v.tensor_copy(padded(wq)[:, :, gg, :], gate_part(0)[:, :, gg, :]).then_inc(s.wpad_done, 1)
                v.tensor_tensor(padded(wc)[:, :, gg, :], gate_part(1)[:, :, gg, :], gate_part(2)[:, :, gg, :],
                                ALU.add).then_inc(s.wpad_done, 1)
            dve.wait_ge(s.rs1_done, 1)
            for b in range(B):
                v.tensor_scalar(qn[:, b, :], xs[:, b, :], mv1[:, b, 0:1], rs1[:, b:b + 1], ALU.subtract, ALU.mult)\
                    .then_inc(s.qn_done, 1)
            for i in range(2):
                dve.wait_ge(s.cT_ps, 4 * i + 4)
                v.tensor_copy(cT[:, 4 * i:4 * i + 4, :], bank[6 + i][:].rearrange("p (b t) -> p b t", t=S))\
                    .then_inc(s.cT_done, 1)
            dve.wait_ge(s.gates_ps, 1)
            dve.wait_ge(s.bias_in, 48)
            v.tensor_scalar(fgt[:], pv_bank[0][BH:128, 0:S], gbias[BH:128, :], None, ALU.add).then_inc(s.fgt_done, 1)
            dve.wait_ge(s.fgt_done, 1)
            v.scalar_tensor_tensor(out=nabs[:], in0=fgt[:], scalar=-1.0, in1=fgt[:], op0=ALU.mult, op1=ALU.min)\
                .then_inc(s.nabs_done, 1)
            dve.wait_ge(s.softplus_done, 1)
            v.scalar_tensor_tensor(out=logf[:], in0=fgt[:], scalar=0.0, in1=nabs[:], op0=ALU.min, op1=ALU.subtract)\
                .then_inc(s.logf_done, 1)
            dve.wait_ge(s.logf_done, 1)
            dve.wait_ge(s.const_zero, 13)
            v.tensor_tensor_scan(lsum[:], ones64[:], logf[:], 0.0, ALU.mult, ALU.add).then_inc(s.lsum_done, 1)
            dve.wait_ge(s.lsum_done, 1)
            v.scalar_tensor_tensor(out=um[0:BH, :], in0=pv_bank[0][0:BH, 0:S], scalar=gbias[0:BH, :], in1=lsum[:],
                                   op0=ALU.add, op1=ALU.subtract).then_inc(s.u_done, 1)
            dve.wait_ge(s.u_done, 1)
            v.tensor_tensor_scan(cm[:], um[0:BH, :], um[0:BH, :], -3e38, ALU.max, ALU.max).then_inc(s.cm_done, 1)
            dve.wait_ge(s.cm_done, 1)
            v.tensor_scalar(um[BH:128, :], cm[:], -1.0, None, ALU.mult).then_inc(s.um_done, 1)
            v.tensor_tensor(mld[:], cm[:], lsum[:], ALU.add).then_inc(s.mld_done, 1)
            dve.wait_ge(s.um_done, 1)
            v.tensor_copy(parts[:, 0, :], um[:]).then_inc(s.part_done, 1)
            dve.wait_ge(s.part_done, 1)
            v.tensor_tensor(um1[:], um[:], parts[:, 0, :], ALU.subtract).then_inc(s.um1_done, 1)
            dve.wait_ge(s.um1_done, 1)
            v.tensor_copy(parts[:, 1, :], um1[:]).then_inc(s.part_done, 1)
            dve.wait_ge(s.part_done, 2)
            v.tensor_tensor(parts[:, 2, :], um1[:], parts[:, 1, :], ALU.subtract).then_inc(s.part_done, 1)
            dve.wait_ge(s.emT_done, 1)
            v.tensor_scalar_add(emTe[:], emT[:], EPS_NORMALIZER).then_inc(s.iota_done, 1)
            dve.wait_ge(s.iota_done, 6)

            def weigh(b):
                for half in range(2):
                    dve.wait_ge(s.dec_done, 2 * b + half + 1)
                    dve.wait_ge(s.qk_ps, 2 * b + half + 1)
                    v.tensor_tensor(cw[:, b % 2, half * 4:half * 4 + 4, :],
                                    qk_bank(b, half)[:].rearrange("p (h t) -> p h t", t=S),
                                    dec[:, b % 2, half * 4:half * 4 + 4, :], ALU.mult).then_inc(s.cw_done, 1)

            def normalise(j):
                p = j % 2
                pv = pv_bank[p][:, 0:2 * NH * (DH + 1)].rearrange("p (i h c) -> p i h c", i=2, c=DH + 1)
                floor = emTe[:, 2 * NH * j:2 * NH * (j + 1)].rearrange("p (i h) -> p i h", h=NH)
                dve.wait_ge(s.pv_ps, 2 * j + 2)
                v.scalar_tensor_tensor(out=den1[:, p, :, :], in0=pv[:, :, :, DH], scalar=EPS_NORMALIZER, in1=floor,
                                       op0=ALU.add, op1=ALU.max).then_inc(s.den1_done, 1)
                v.tensor_scalar(den2[:, p, :, :], pv[:, :, :, DH], -1.0, EPS_NORMALIZER, ALU.mult, ALU.add)\
                    .then_inc(s.den2_done, 1)
                dve.wait_ge(s.den1_done, j + 1)
                dve.wait_ge(s.den2_done, j + 1)
                v.tensor_tensor(den[:, p, :, :], den1[:, p, :, :], den2[:, p, :, :], ALU.max).then_inc(s.den_done, 1)
                dve.wait_ge(s.den_done, j + 1)
                v.reciprocal(rden[:, p, :, :], den[:, p, :, :]).then_inc(s.rden_done, 1)
                dve.wait_ge(s.rden_done, j + 1)
                v.tensor_tensor(hn[:, p, :, :].rearrange("p i (h c) -> p (i h) c", c=DH),
                                pv.rearrange("p i h c -> p (i h) c")[:, :, 0:DH],
                                rden[:, p, :, :].rearrange("p i h -> p (i h)").unsqueeze(2)
                                .to_broadcast([128, 2 * NH, DH]), ALU.mult).then_inc(s.hn_done, 1)
                dve.wait_ge(s.hn_done, j + 1)
                for i in range(2):
                    v.bn_stats(st2[:, p, i, :], hn[:, p, i, :]).then_inc(s.st2_done, 1)
                for i in range(2):
                    dve.wait_ge(s.st2_done, 2 * j + i + 1)
                    v.bn_aggr(mv2[:, 2 * j + i, :], st2[:, p, i, :]).then_inc(s.mv2_done, 1)
                dve.wait_ge(s.mv2_done, 2 * j + 2)
                v.tensor_scalar_add(ve2[:, 2 * j:2 * j + 2], mv2[:, 2 * j:2 * j + 2, 1], EPS_LN).then_inc(s.ve2_done, 1)
                for i in range(2):
                    v.scalar_tensor_tensor(out=hl[:, p, i, :], in0=hn[:, p, i, :], scalar=mv2[:, 2 * j + i, 0:1],
                                           in1=lnsb[:], op0=ALU.subtract, op1=ALU.mult).then_inc(s.hl_done, 1)

            def residual(j):
                p = j % 2
                dve.wait_ge(s.rs2_done, j + 1)
                dve.wait_ge(s.hl_done, 2 * j + 2)
                for i in range(2):
                    b = 2 * j + i
                    v.scalar_tensor_tensor(out=x2[:, b, :], in0=hl[:, p, i, :], scalar=rs2[:, b:b + 1], in1=xs[:, b, :],
                                           op0=ALU.mult, op1=ALU.add).then_inc(s.x2_done, 1)
                for i in range(2):
                    dve.wait_ge(s.x2_done, 2 * j + i + 1)
                    v.bn_stats(st3[:, p, i, :], x2[:, 2 * j + i, :]).then_inc(s.st3_done, 1)
                for i in range(2):
                    dve.wait_ge(s.st3_done, 2 * j + i + 1)
                    v.bn_aggr(mv3[:, 2 * j + i, :], st3[:, p, i, :]).then_inc(s.mv3_done, 1)
                dve.wait_ge(s.mv3_done, 2 * j + 2)
                v.tensor_scalar_add(ve3[:, 2 * j:2 * j + 2], mv3[:, 2 * j:2 * j + 2, 1], EPS_LN).then_inc(s.ve3_done, 1)

            def norm2(j):
                dve.wait_ge(s.rs3_done, j + 1)
                for b in (2 * j, 2 * j + 1):
                    v.tensor_scalar(xn[:, b, :], x2[:, b, :], mv3[:, b, 0:1], rs3[:, b:b + 1], ALU.subtract, ALU.mult)\
                        .then_inc(s.xn_done, 1)

            def choose(j):
                pair = slice(2 * j, 2 * j + 2)
                dve.wait_ge(s.score_ps, j + 1)
                for i in range(2):
                    v.max(top[:, 2 * j + i, :], misc[:, 256 + 8 * i:264 + 8 * i]).then_inc(s.top_done, 1)
                for i in range(2):
                    b = 2 * j + i
                    dve.wait_ge(s.top_done, b + 1)
                    v.max_index(topi[:, b, :], top[:, b, :], misc[:, 256 + 8 * i:264 + 8 * i]).then_inc(s.topi_done, 1)
                dve.wait_ge(s.topi_done, 2 * j + 2)
                v.tensor_copy(topf[:, pair, :], topi[:, pair, 0:2]).then_inc(s.topf_done, 1)
                dve.wait_ge(s.topf_done, j + 1)
                v.tensor_tensor(ohk[:, pair, :, :].rearrange("p b k e -> p (b k) e"),
                                iota[:, 0:NE].unsqueeze(1).to_broadcast([128, 4, NE]),
                                topf[:, pair, :].rearrange("p b k -> p (b k)").unsqueeze(2).to_broadcast([128, 4, NE]),
                                ALU.is_equal).then_inc(s.oh_done, 1)
                dve.wait_ge(s.oh_done, j + 1)
                v.tensor_tensor(maskb[:, pair, :], ohk[:, pair, 0, :], ohk[:, pair, 1, :], ALU.add).then_inc(s.mask_done, 1)
                dve.wait_ge(s.mask_done, j + 1)
                for b in (2 * j, 2 * j + 1):
                    if b >= 1:
                        dve.wait_ge(s.pref_done, b)
                    v.tensor_tensor(prefb[:, b + 1, :], prefb[:, b, :], maskb[:, b, :], ALU.add).then_inc(s.pref_done, 1)

            def route(j):
                pair = slice(2 * j, 2 * j + 2)
                rk = misc[:, 288:288 + 2 * NE].rearrange("p (i e) -> p i e", e=NE)
                dve.wait_ge(s.rank_ps, j + 1)
                v.tensor_scalar(beyond[:], rk, float(MAIN), float(GAP), ALU.is_ge, ALU.mult).then_inc(s.beyond_done, 1)
                dve.wait_ge(s.beyond_done, j + 1)
                v.tensor_tensor(beyond[:], beyond[:], rk, ALU.add).then_inc(s.place_done, 1)
                dve.wait_ge(s.place_done, j + 1)
                v.tensor_tensor(place[:], beyond[:], ebase[:].unsqueeze(1).to_broadcast([128, 2, NE]), ALU.add)\
                    .then_inc(s.base_done, 1)
                dve.wait_ge(s.base_done, j + 1)
                v.tensor_tensor(placed[:], ohk[:, pair, :, :], place[:].unsqueeze(2).to_broadcast([128, 2, 2, NE]),
                                ALU.mult).then_inc(s.placed_done, 1)
                dve.wait_ge(s.placed_done, j + 1)
                v.tensor_reduce(sl[:, pair, :], placed[:], axis=AX.X, op=ALU.add).then_inc(s.sl_done, 1)
                dve.wait_ge(s.sl_done, j + 1)
                v.tensor_scalar(slf[:, pair, :], sl[:, pair, :], 1.0 / 128, -63.5 / 128, ALU.mult, ALU.add)\
                    .then_inc(s.slf_done, 1)
                dve.wait_ge(s.slf_done, j + 1)
                v.tensor_scalar(cf[:, pair, :], slf[:, pair, :], ROUND, -ROUND, ALU.add, ALU.add)\
                    .then_inc(s.cf_done, 1)
                dve.wait_ge(s.cf_done, j + 1)
                v.scalar_tensor_tensor(out=rf[:, pair, :], in0=cf[:, pair, :], scalar=-128.0, in1=sl[:, pair, :],
                                       op0=ALU.mult, op1=ALU.add).then_inc(s.rf_done, 1)
                dve.wait_ge(s.rf_done, j + 1)
                for b in (2 * j, 2 * j + 1):
                    for k in range(2):
                        v.tensor_scalar(ohb[:, 2 * b + k, :], iotab[:], rf[:, b, k:k + 1], None, ALU.is_equal)\
                            .then_inc(s.oha_done, 1)
                        v.tensor_scalar(oha[:, 2 * b + k, :], iotab[:, 0:NC], cf[:, b, k:k + 1], tokval[:, b:b + 1],
                                        ALU.is_equal, ALU.mult).then_inc(s.oha_done, 1)

            NP = B // 2
            for j in range(NP + 2):
                if j < NP:
                    weigh(2 * j)
                if 0 <= j - 1 < NP:
                    normalise(j - 1)
                if 0 <= j - 3 < NP:
                    route(j - 3)
                if j < NP:
                    weigh(2 * j + 1)
                if 0 <= j - 1 < NP:
                    residual(j - 1)
                if 0 <= j - 2 < NP:
                    choose(j - 2)
                if 0 <= j - 1 < NP:
                    norm2(j - 1)
            dve.wait_ge(s.rank_ps, NP)
            v.tensor_reduce(cntf[:], misc[:, 320:320 + NE], axis=AX.X, op=ALU.max).then_inc(s.cnt_done, 1)
            route(NP - 1)
            dve.wait_ge(s.cnt_done, 1)
            v.tensor_copy(cnti[:], cntf[:]).then_inc(s.cnti_done, 1)
            lists = lists_bank[:, 0:NC]
            dve.wait_ge(s.lists_ps, 1)
            v.scalar_tensor_tensor(out=padterm[:], in0=lists, scalar=0.0, in1=padval[:].rearrange("p a c -> p (a c)"),
                                   op0=ALU.is_equal, op1=ALU.mult).then_inc(s.padterm_done, 1)
            dve.wait_ge(s.padterm_done, 1)
            v.scalar_tensor_tensor(out=ids[:], in0=lists, scalar=float(2 * T), in1=padterm[:], op0=ALU.add, op1=ALU.add)\
                .then_inc(s.ids_done, 1)

            def split_x(e):
                dve.wait_ge(s.xT_ps, e + 1)
                if e >= 1:
                    dve.wait_ge(s.l1_ps, MC * e)
                v.tensor_copy(xhi[:], bank[5][:, 0:MAIN]).then_inc(s.xhi_done, 1)
                dve.wait_ge(s.xhi_done, e + 1)
                v.tensor_tensor(xlo[:], bank[5][:, 0:MAIN], xhi[:].bitcast(F32), ALU.subtract).then_inc(s.xlo_done, 1)

            def split_g(e, layer):
                gd, hd, ld, g, gh, gl = ((s.gelu1_done, s.g1h_done, s.g1l_done, g1, g1h, g1l),
                                         (s.gelu2_done, s.g2h_done, s.g2l_done, g2, g2h, g2l))[layer - 1]
                for m in range(MC):
                    dve.wait_ge(gd, MC * e + m + 1)
                    v.tensor_copy(gh[:, m, :], g[:, m, :]).then_inc(hd, 1)
                    dve.wait_ge(hd, MC * e + m + 1)
                    v.tensor_tensor(gl[:, m, :], g[:, m, :], gh[:, m, :].bitcast(F32), ALU.subtract).then_inc(ld, 1)

            def weights_lo2(e):
                dve.wait_ge(s.whi_done, e + 1)
                c = slice(HID, HID + MC * HID)
                v.tensor_tensor(wlo[e % 2][:, c], wraw[:, e, c], whi[e % 2][:, c].bitcast(F32), ALU.subtract)\
                    .then_inc(s.wlo_done, 1)

            def rows_y(e):
                dve.wait_ge(s.y_ps, e + 1)
                if e >= 2:
                    dve.wait_ge(s.added, 48 * (e - 1))
                v.tensor_copy(ys[:, e % 2, :, :], bank[6][:, 0:384].rearrange("p (c d) -> p c d", d=D)).then_inc(s.ys_done, 1)
            weights_lo2(0)
            split_x(0)
            split_g(0, 1)
            weights_lo2(1)
            for e in range(NE):
                if e >= 1 and e + 1 < NE:
                    weights_lo2(e + 1)
                if e + 1 < NE:
                    split_x(e + 1)
                split_g(e, 2)
                if e >= 1:
                    rows_y(e - 1)
                if e + 1 < NE:
                    split_g(e + 1, 1)
                if e == 2:
                    most = most_tokens(dve)
            rows_y(NE - 1)

            with dve.If(most > MAIN):
                with dve.Fori(0, NE) as e:
                    for c in range(STEPS):
                        n = STEPS * e + c + 1
                        dve.wait_ge(s.r_turn, 3 * n - 2)
                        v.memset(turnd[:], 0.0)
                        v.tensor_copy(rbias[:, 0:MC], smt[:, bass.ds(MC * e, MC)])
                        v.tensor_copy(rbias[:, MC:2 * MC], smt[:, bass.ds(NE * MC + MC * e, MC)])
                        v.tensor_copy(rbias[:, 2 * MC:2 * MC + 1], smt[:, bass.ds(2 * NE * MC + e, 1)]).then_inc(s.r_bias, 1)
                        v.tensor_copy(rids[:], ids[:, bass.ds(CHUNKS * e + 3 + RC * c, RC)]).then_inc(s.r_ids, 1)
                        dve.wait_ge(s.r_xT, n)
                        v.tensor_copy(xhi[:, 0:REST], bank[5][:, 0:REST]).then_inc(s.r_xhi, 1)
                        dve.wait_ge(s.r_xhi, n)
                        v.tensor_tensor(xlo[:, 0:REST], bank[5][:, 0:REST], xhi[:, 0:REST].bitcast(F32), ALU.subtract)\
                            .then_inc(s.r_xlo, 1)
                        for gd, hd, ld, gt, gh, gl in ((s.r_gelu1, s.r_g1h, s.r_g1l, g1, g1h, g1l),
                                                       (s.r_gelu2, s.r_g2h, s.r_g2l, g2, g2h, g2l)):
                            dve.wait_ge(gd, MC * n)
                            v.tensor_copy(gh[:, :, 0:REST], gt[:, :, 0:REST]).then_inc(hd, 1)
                            dve.wait_ge(hd, n)
                            v.tensor_tensor(gl[:, :, 0:REST], gt[:, :, 0:REST], gh[:, :, 0:REST].bitcast(F32),
                                            ALU.subtract).then_inc(ld, 1)
                        dve.wait_ge(s.r_l3, n)
                        dve.wait_ge(s.r_bias, n)
                        v.tensor_scalar(yT[:, 0:REST], bank[4][:, 0:REST], rbias[:, 2 * MC:2 * MC + 1], 0.5,
                                        ALU.add, ALU.mult).then_inc(s.r_yT, 1)
                        dve.wait_ge(s.r_y, n)
                        v.tensor_copy(ys[:, 0, 0:RC, :], bank[6][:, 0:REST].rearrange("p (c d) -> p c d", d=D))\
                            .then_inc(s.r_ys, 1)

        @block.tensor
        def _(pe):
            t = nc.tensor
            pe.wait_ge(s.const_done, 1)
            pe.wait_ge(s.small_in, 16 * 10)
            t.transpose(bank[0][:, 0:128], sm[:], identf[:]).then_inc(s.sm_T, 1)
            for b in range(B):
                pe.wait_ge(ctx_in[b // 4], 16)
                t.transpose(bank[6 + b // 4][:, (b % 4) * S:(b % 4 + 1) * S], cs_in[:, b, :], identf[:]).then_inc(s.cT_ps, 1)
            for b in range(B):
                pe.wait_ge(s.qn_done, b + 1)
                t.transpose(arg_bank[b // 4][:, (b % 4) * S:(b % 4 + 1) * S], qn[:, b, :], identf[:]).then_inc(s.qT_ps, 1)
            pe.wait_ge(s.wpad_done, 4)
            pe.wait_ge(s.qT_done, 2)
            pe.wait_ge(s.cT_done, 2)
            for b in range(B):
                t.matmul(pv_bank[0][:, 0:S], wc[:, 2 * BH * b:2 * BH * (b + 1)], cT[:, b, :], start=(b == 0), stop=False)
                last = t.matmul(pv_bank[0][:, 0:S], wq[:, 2 * BH * b:2 * BH * (b + 1)], qT[:, b, :],
                                start=False, stop=(b == B - 1))
            last.then_inc(s.gates_ps, 1)

            def logits(b):
                pe.wait_ge(s.qbd_done, b + 1)
                if b == 0:
                    pe.wait_ge(s.smt_done, 1)
                for half in range(2):
                    if 2 * b + half >= 3:
                        pe.wait_ge(s.cw_done, 2 * b + half - 2)
                    t.matmul(qk_bank(b, half)[:], cT[:, b, :],
                             qbd[:, b % 2, half * 4:half * 4 + 4, :].rearrange("p h t -> p (h t)"),
                             start=True, stop=True).then_inc(s.qk_ps, 1)

            def exponents(b):
                if b == 0:
                    pe.wait_ge(s.max_in, 16 * (3 + B))
                    pe.wait_ge(s.rh_done, 1)
                    pe.wait_ge(s.const_done, 7)
                for half in range(2):
                    if b >= 1:
                        pe.wait_ge(s.dec_done, 2 * b + half - 1)
                    dst = arg_bank[half][:].rearrange("p (h t) -> p h t", t=S)
                    t.matmul(dst, LT[:, b, :], RH[:, NH * b + 4 * half:NH * b + 4 * half + 4, :], start=True, stop=False)
                    t.matmul(dst, identb[:], negb[:].unsqueeze(1).to_broadcast([128, 4, S]), start=False, stop=True)\
                        .then_inc(s.arg_ps, 1)

            def values(b):
                if b % 2 == 0 and b >= 4:
                    pe.wait_ge(s.hn_done, b // 2 - 1)
                if b == 0:
                    pe.wait_ge(s.v1_done, 1)
                for h in range(NH):
                    pe.wait_ge(s.cw_done, 2 * b + h // 4 + 1)
                    c = (DH + 1) * (NH * (b % 2) + h)
                    last = t.matmul(pv_bank[b // 2 % 2][:, c:c + DH + 1], cw[:, b % 2, h, :], v1[:, b, h, :],
                                    start=True, stop=True)
                last.then_inc(s.pv_ps, 1)

            def xn_transpose(j):
                pe.wait_ge(s.xn_done, 2 * j + 2)
                if j >= 1:
                    pe.wait_ge(s.place_done, j)
                else:
                    pe.wait_ge(s.emT_done, 1)
                for i in range(2):
                    last = t.transpose(misc[:, i * S:(i + 1) * S], xn[:, 2 * j + i, :], identf[:])
                last.then_inc(s.xnT_ps, 1)

            def scores(j):
                pe.wait_ge(s.xnT_done, j + 1)
                for i in range(2):
                    last = t.matmul(misc[:, 256 + 8 * i:264 + 8 * i], xnT[:, i, :], smt[:, 72:80], start=True, stop=True)
                last.then_inc(s.score_ps, 1)

            def ranks(j):
                pe.wait_ge(s.pref_done, 2 * j + 2)
                pair = slice(2 * j, 2 * j + 2)
                t.matmul(misc[:, 288:288 + 2 * NE], trib[:], maskb[:, pair, :].rearrange("p b e -> p (b e)"),
                         start=True, stop=False)
                last = t.matmul(misc[:, 288:288 + 2 * NE], onesb[:], prefb[:, pair, :].rearrange("p b e -> p (b e)"),
                                start=False, stop=True)
                if j == B // 2 - 1:
                    last = t.matmul(misc[:, 320:320 + NE], onesb[:], prefb[:, B, :], start=True, stop=True)
                last.then_inc(s.rank_ps, 1)

            def lists(j):
                for i in range(4):
                    n = 4 * j + i
                    pe.wait_ge(s.oha_done, 2 * (n + 1))
                    last = t.matmul(lists_bank[:, 0:NC], ohb[:, n, :], oha[:, n, :],
                                    start=(n == 0), stop=(n == 2 * B - 1))
                if j == B // 2 - 1:
                    last.then_inc(s.lists_ps, 1)
            NP = B // 2
            logits(0)
            for j in range(NP + 2):
                if j < NP:
                    if j > 0:
                        logits(2 * j)
                    exponents(2 * j)
                if 0 <= j - 1 < NP:
                    values(2 * j - 1)
                if j == 0:
                    pe.wait_ge(s.em_done, 1)
                    t.transpose(misc[:, 0:BH], em[:], identf[0:BH, 0:BH]).then_inc(s.emT_ps, 1)
                if 0 <= j - 3 < NP:
                    ranks(j - 3)
                if 0 <= j - 2 < NP:
                    xn_transpose(j - 2)
                if j < NP:
                    logits(2 * j + 1)
                    exponents(2 * j + 1)
                    values(2 * j)
                if 0 <= j - 2 < NP:
                    scores(j - 2)
            ranks(NP - 1)
            for j in range(NP):
                lists(j)

            def x_transpose(e):
                pe.wait_ge(gathered[e % 2], 48 * (e // 2 + 1))
                if e >= 1:
                    pe.wait_ge(s.xlo_done, e)
                for c in range(3):
                    n = min(128, MAIN - 128 * c)
                    last = t.transpose(bank[5][:, 128 * c:128 * c + n], xg[0:n, e % 2, c, :], identf[0:n, 0:n])
                last.then_inc(s.xT_ps, 1)

            def product(dst, e, layer, m, ks, ahi, alo):
                p = e % 2
                n = 0
                for k in range(ks):
                    for w, act_ in ((whi, ahi), (wlo, ahi), (whi, alo)):
                        last = t.matmul(dst, wcol(w, p, layer, k, m), act_(k), start=(n == 0), stop=(n == 3 * ks - 1))
                        n += 1
                return last

            def layer1(e):
                pe.wait_ge(s.xlo_done, e + 1)
                pe.wait_ge(s.wlo13_done, 2 * e + 2)
                for m in range(MC):
                    if e >= 1:
                        pe.wait_ge(s.gelu2_done, MC * (e - 1) + m + 1)
                    product(bank[m][:, 0:MAIN], e, 1, m, 1, lambda k: xhi[:], lambda k: xlo[:]).then_inc(s.l1_ps, 1)

            def layer2(e):
                pe.wait_ge(s.g1l_done, MC * (e + 1))
                pe.wait_ge(s.wlo_done, e + 1)
                for m in range(MC):
                    product(bank[m][:, 0:MAIN], e, 2, m, MC, lambda k: g1h[:, k, :], lambda k: g1l[:, k, :])\
                        .then_inc(s.l2_ps, 1)
                    if m == 0 and e + 1 < NE:
                        x_transpose(e + 1)
                    if m == 1 and e >= 1:
                        y_transpose(e - 1)

            def layer3(e):
                pe.wait_ge(s.g2l_done, MC * (e + 1))
                if e >= 1:
                    pe.wait_ge(s.yT_done, e)
                product(bank[4][:, 0:MAIN], e, 3, 0, MC, lambda k: g2h[:, k, :], lambda k: g2l[:, k, :])\
                    .then_inc(s.l3_ps, 1)

            def y_transpose(e):
                pe.wait_ge(s.yT_done, e + 1)
                if e >= 1:
                    pe.wait_ge(s.ys_done, e)
                for c in range(3):
                    n = min(128, MAIN - 128 * c)
                    last = t.transpose(bank[6][0:n, 128 * c:128 * c + D], yT[:, 128 * c:128 * c + n], identf[:])
                last.then_inc(s.y_ps, 1)
            x_transpose(0)
            layer1(0)
            for e in range(NE):
                layer2(e)
                if e + 1 < NE:
                    layer1(e + 1)
                layer3(e)
                if e == 2:
                    most = most_tokens(pe)
            y_transpose(NE - 1)

            with pe.If(most > MAIN):
                with pe.Fori(0, NE) as e:
                    for c in range(STEPS):
                        n = STEPS * e + c + 1
                        pe.wait_ge(s.r_gathered, 16 * RC * n)
                        for j in range(RC):
                            last = t.transpose(bank[5][:, 128 * j:128 * j + 128], xg[:, 0, j, :], identf[:])
                        last.then_inc(s.r_xT, 1)
                        pe.wait_ge(s.r_xlo, n)
                        if c == 0:
                            pe.wait_ge(s.r_wlo, e + 1)
                        for m in range(MC):
                            last = product(bank[m][:, 0:REST], 0, 1, m, 1, lambda k: xhi[:, 0:REST], lambda k: xlo[:, 0:REST])
                        last.then_inc(s.r_l1, 1)
                        pe.wait_ge(s.r_g1l, n)
                        for m in range(MC):
                            last = product(bank[m][:, 0:REST], 0, 2, m, MC, lambda k: g1h[:, k, 0:REST],
                                           lambda k: g1l[:, k, 0:REST])
                        last.then_inc(s.r_l2, 1)
                        pe.wait_ge(s.r_g2l, n)
                        product(bank[4][:, 0:REST], 0, 3, 0, MC, lambda k: g2h[:, k, 0:REST],
                                lambda k: g2l[:, k, 0:REST]).then_inc(s.r_l3, 1)
                        pe.wait_ge(s.r_yT, n)
                        for j in range(RC):
                            last = t.transpose(bank[6][:, 128 * j:128 * j + D], yT[:, 128 * j:128 * j + 128], identf[:])
                        last.then_inc(s.r_y, 1)


NAMES = ["x", "ctx_1024", "L0_xattn_igate_w", "L0_xattn_igate_b", "L0_xattn_fgate_w", "L0_xattn_fgate_b",
         "L0_xattn_ln_scale", "L0_ffn_expert_tokens", "L0_ffn_W1", "L0_ffn_b1", "L0_ffn_W2", "L0_ffn_b2",
         "L0_ffn_W3", "L0_ffn_b3"]


def kernel(**inputs):
    import numpy as _np
    import concourse.bacc as _bacc
    from concourse import mybir as _mybir
    from concourse.bass_utils import run_bass_kernel_spmd as _run

    nc = _bacc.Bacc("TRN2", target_bir_lowering=False, num_devices=1)
    arrays, args = {}, []
    for name in NAMES:
        a = _np.ascontiguousarray(inputs[name])
        arrays[f"in_{name}"] = a
        args.append(nc.dram_tensor(f"in_{name}", a.shape, _mybir.dt.from_np(a.dtype), kind="ExternalInput").ap())
    out = nc.dram_tensor("out_rows", (T + PAD, D), F32, kind="ExternalOutput").ap()
    build(nc, *args, out)
    r = _run(nc, [arrays], core_ids=[0])
    return r.results[0]["out_rows"][0:T].reshape(B, S, D)
```

```python
from collections import namedtuple
from contextlib import ExitStack

import numpy as np
import concourse.bass as bass
from concourse import mybir

F32 = mybir.dt.float32
F32R = mybir.dt.float32r
BF16 = mybir.dt.bfloat16
F16 = mybir.dt.float16
I32 = mybir.dt.int32
U32 = mybir.dt.uint32
ALU = mybir.AluOpType
ACT = mybir.ActivationFunctionType
AX = mybir.AxisListType

B, S, D = 8, 128, 128
NH = 8
DH = D // NH
BH = B * NH
NE = 8
HID = 512
MC = HID // 128
T = B * S
EPS_NORMALIZER = 1e-6
EPS_LN = 1e-5
NEG = -1e38

MAIN = 320
CHUNKS = 9
GAP = 3 * 128 - MAIN
PLACES = CHUNKS * 128
RC = 2
REST = RC * 128
WARM = {"inputs": 8, "gate weights": 2, "gate scans": 8, "gate rows": 14, "last choice": 6, "token lists": 14, "first split": 5}
PAD = 3 * 128
ROUND = 1.5 * 2.0 ** 23
NC = NE * CHUNKS
STEPS = (CHUNKS - 3) // RC
LAYER = {1: slice(0, HID), 2: slice(HID, HID + MC * HID), 3: slice(HID + MC * HID, HID + MC * HID + MC * D)}
WCOLS = HID + MC * HID + MC * D


def build(nc, x, ctx, igw, igb, fgw, fgb, lns, et, W1, b1, W2, b2, W3, b3, out):
    es = ExitStack()
    with es:
        def sb(name, shape, dt=F32):
            return es.enter_context(nc.sbuf_tensor(name, shape, dt))

        def sem(name):
            return es.enter_context(nc.semaphore(name))

        xnd = nc.dram_tensor("xn_rows", (T + PAD, D), F32, kind="Internal").ap()

        wraw = sb("wraw", [128, NE, WCOLS])
        whi = [sb("whi0", [128, WCOLS], F32R)]
        wlo = [sb("wlo0", [128, WCOLS], F32R)]
        identf = sb("identf", [128, 128])
        identb = sb("identb", [128, 128], BF16)
        negb = sb("negb", [128, 128], BF16)
        trib = sb("trib", [128, 128], BF16)
        onesb = sb("onesb", [128, 128], BF16)
        iota = sb("iota", [128, 128])
        iotab = sb("iotab", [128, 128], F16)
        hmask = sb("hmask", [128, NH])
        minus_half = sb("minus_half", [128, NH])
        tokval = sb("tokval", [128, B])
        padval = sb("padval", [128, NC // 3, 3])
        ebase = sb("ebase", [128, NE])
        zrow = sb("zrow", [128, D])
        ones64 = sb("ones64", [BH, S])
        onecol = sb("onecol", [128, 1])
        gw = sb("gw", [48, 128])
        gwt = sb("gwt", [128, 48])
        sm = sb("sm", [80, 128])
        smt = sb("smt", [128, 80])
        gbias = sb("gbias", [128, 1])
        lnsb = sb("lnsb", [128, D])
        b3h = sb("b3h", [128, NE])
        ohk = sb("ohk", [128, B, 2, NE])
        maskb = sb("maskb", [128, B, NE], BF16)
        prefb = sb("prefb", [128, B + 1, NE], BF16)
        top = sb("top", [128, B, 8])
        topi = sb("topi", [128, B, 8], U32)
        topf = sb("topf", [128, B, 2])
        beyond = sb("beyond", [128, 2, NE])
        place = sb("place", [128, 2, NE])
        placed = sb("placed", [128, 2, 2, NE])
        sl = sb("sl", [128, B, 2])
        slf = sb("slf", [128, B, 2])
        cf = sb("cf", [128, B, 2])
        rf = sb("rf", [128, B, 2])
        padterm = sb("padterm", [128, NC])
        ids = sb("ids", [128, NC], U32)
        cntf = sb("cntf", [128, 1])
        cnti = sb("cnti", [128, 1], I32)
        rids = sb("rids", [128, RC], U32)
        rbias = sb("rbias", [128, 2 * MC + 1])
        turn = sb("turn", [128, 1])
        turnd = sb("turnd", [128, 1])

        attn = ExitStack()

        def at(name, shape, dt=F32):
            return attn.enter_context(nc.sbuf_tensor(name, shape, dt))

        xs = at("xs", [128, B, D])
        cs_in = at("cs_in", [128, B, D])
        qn = at("qn", [128, B, D])
        qT = at("qT", [128, B, S])
        cT = at("cT", [128, B, S])
        v1 = at("v1", [128, B, NH, DH + 1])
        st1 = at("st1", [128, B, 6])
        mv1 = at("mv1", [128, B, 2])
        ve1 = at("ve1", [128, B])
        rs1 = at("rs1", [128, B])
        emT = at("emT", [128, BH])
        emTe = at("emTe", [128, BH])
        em = at("em", [BH, S])
        um = at("um", [128, S])
        parts = at("parts", [128, 3, S], BF16)
        LT = at("LT", [3 * NH + 3, B, S], BF16)
        RH = at("RH", [3 * NH + 3, BH, S], BF16)
        delta = at("delta", [3 * NH, NH])
        qbd = at("qbd", [128, 2, NH, S])
        dec = at("dec", [128, 2, NH, S])
        cw = dec
        den1 = at("den1", [128, 2, 2, NH])
        den2 = at("den2", [128, 2, 2, NH])
        den = at("den", [128, 2, 2, NH])
        rden = at("rden", [128, 2, 2, NH])
        gates = ExitStack()

        def gt(name, shape, dt=F32):
            return gates.enter_context(nc.sbuf_tensor(name, shape, dt))
        fgt = gt("fgt", [BH, S])
        nabs = gt("nabs", [BH, S])
        expn = gt("expn", [BH, S])
        logf = gt("logf", [BH, S])
        lsum = gt("lsum", [BH, S])
        cm = gt("cm", [BH, S])
        mld = gt("mld", [BH, S])
        um1 = gt("um1", [128, S])
        gates.close()
        hn = at("hn", [128, 2, 2, D])
        hl = at("hl", [128, 2, 2, D])
        st2 = at("st2", [128, 2, 2, 6])
        mv2 = at("mv2", [128, B, 2])
        ve2 = at("ve2", [128, B])
        rs2 = at("rs2", [128, B])
        x2 = at("x2", [128, B, D])
        st3 = at("st3", [128, 2, 2, 6])
        mv3 = at("mv3", [128, B, 2])
        ve3 = at("ve3", [128, B])
        rs3 = at("rs3", [128, B])
        xn = qn
        xnT = at("xnT", [128, 2, S])
        mark = ExitStack()
        wq = mark.enter_context(nc.sbuf_tensor("wq", [128, B * (BH * 2 + NH)], F32))
        wc = mark.enter_context(nc.sbuf_tensor("wc", [128, B * (BH * 2 + NH)], F32))
        mark.close()
        ohb = at("ohb", [128, 2 * B, 128], F16)
        oha = at("oha", [128, 2 * B, NC], F16)
        attn.close()
        whi.append(sb("whi1", [128, WCOLS], F32R))
        wlo.append(sb("wlo1", [128, WCOLS], F32R))
        xg = sb("xg", [128, 2, 3, D])
        xhi = sb("xhi", [128, MAIN], F32R)
        xlo = sb("xlo", [128, MAIN], F32R)
        g1 = sb("g1", [128, MC, MAIN])
        g1h = sb("g1h", [128, MC, MAIN], F32R)
        g1l = sb("g1l", [128, MC, MAIN], F32R)
        g2 = sb("g2", [128, MC, MAIN])
        g2h = sb("g2h", [128, MC, MAIN], F32R)
        g2l = sb("g2l", [128, MC, MAIN], F32R)
        yT = sb("yT", [128, MAIN])
        ys = sb("ys", [128, 2, 3, D])

        bank = [es.enter_context(nc.psum_tensor(f"bank{i}", [128, 512], F32)) for i in range(8)]

        names = """
        gw_in gw_T gwt_done x_in0 x_in1 ctx_in0 ctx_in1 small_in bias_in w_in0 w_in1 w_in2 w_in3 w_in4 w_in5 w_in6 w_in7
        ones_done const_zero const_done iota_done ve1_done rs1_done st1_done mv1_done qn_done sm_T smt_done b3h_done
        qT_ps cT_ps qT_done cT_done wq_zero wpad_done v1_done gates_ps
        fgt_done nabs_done expn_done softplus_done logf_done lsum_done u_done cm_done mld_done um_done em_done
        um1_done part_done emT_ps max_in lt0_in lt1_in lt_in emT_done emTe_done delta_done rh_done lt_ones
        qbd_done qk_ps arg_ps dec_done cw_done pv_ps den1_done den2_done den_done rden_done hn_done st2_done mv2_done
        ve2_done rs2_done hl_done x2_done st3_done mv3_done ve3_done rs3_done xn_done xnT_ps xnT_done score_ps
        top_done topi_done topf_done oh_done mask_done pref_done rank_ps beyond_done place_done base_done placed_done
        sl_done slf_done cf_done rf_done ohb_pool oha_pool onehots_dve lists_ps padterm_done ids_done cnt_done cnti_done
        xn_out x2_out gathered0 gathered1 whi1_done whi2_done whi3_done wlo1_done wlo2_done wlo3_done xT_ps xhi_done xlo_done l1_ps gelu1_done g1h_done
        g1l_done l2_ps gelu2_done g2h_done g2l_done l3_ps yT_done y_ps ys_done added
        r_turn r_whi r_wlo r_ids r_bias r_gathered r_xT r_xhi r_xlo r_l1 r_gelu1 r_g1h r_g1l
        r_l2 r_gelu2 r_g2h r_g2l r_l3 r_yT r_y r_ys r_added
        """.split()
        s = namedtuple("Semaphores", names)(*[sem(n) for n in names])
        x_in = [s.x_in0, s.x_in1]
        ctx_in = [s.ctx_in0, s.ctx_in1]
        gathered = [s.gathered0, s.gathered1]
        w_in = [s.w_in0, s.w_in1, s.w_in2, s.w_in3, s.w_in4, s.w_in5, s.w_in6, s.w_in7]

        def wcol(w, p, layer, k, m):
            width = D if layer == 3 else HID
            c = LAYER[layer].start + k * width + m * 128
            return w[p][:, c:c + 128]

        def most_tokens(engine):
            engine.wait_ge(s.cnti_done, 1)
            return engine.value_load(cnti[0:1, 0:1], min_val=0, max_val=T)

        def qk_bank(b, half):
            return bank[(2 * b + half) % 3]

        arg_bank = bank[3:5]
        pv_bank = bank[5:7]
        misc = bank[7]
        lists_bank = bank[0]

        def xnT_bank(j):
            return misc if j < B // 2 - 2 else bank[1]

        def y_bank(e, c):
            return bank[6] if e < NE - 1 else bank[c]

        def score_bank(j):
            return misc if j < B // 2 - 2 else bank[2]

        block = es.enter_context(nc.Block())

        @block.sync
        def _(sp):
            half = B // 2
            for i in range(2):
                sp.dma_start(xs[:, i * half:(i + 1) * half, :],
                             x[i * half:(i + 1) * half].rearrange("b s d -> s b d")).then_inc(x_in[i], 16)
                sp.dma_start(cs_in[:, i * half:(i + 1) * half, :],
                             ctx[i * half:(i + 1) * half].rearrange("b s d -> s b d")).then_inc(ctx_in[i], 16)
            for lo, rows, src in ((0, NE * MC, b1.rearrange("e (m p) -> (e m) p", p=128)),
                                  (32, NE * MC, b2.rearrange("e (m p) -> (e m) p", p=128)),
                                  (64, NE, b3), (72, NE, et)):
                sp.dma_start(sm[lo:lo + rows, :], src).then_inc(s.small_in, 16)
            sp.wait_ge(s.small_in, 16 * 4)
            for e in range(NE):
                if e == 2:
                    for q in range(3):
                        sp.wait_ge(s.part_done, q + 1)
                        sp.dma_start(RH[3 * NH + q:3 * NH + q + 1, :, :], parts[BH:128, q, :]).then_inc(s.max_in, 16)
                    sp.wait_ge(s.lt_ones, 1)
                    sp.dma_start(LT[0:3 * NH, 0, :], parts[0:NH, :, :]).then_inc(s.lt0_in, 16)
                    for b in range(1, B):
                        sp.dma_start(LT[0:3 * NH, b, :], parts[NH * b:NH * b + NH, :, :]).then_inc(s.lt1_in if b == 1 else s.lt_in, 16)
                    sp.wait_ge(s.max_in, 16 * 3)
                    sp.wait_ge(s.lt_in, 16 * (B - 2))
                sp.dma_start(wraw[:, e, 0:HID], W1[e]).then_inc(w_in[e], 16)
                sp.dma_start(wraw[:, e, HID:HID + MC * HID].rearrange("p (k n) -> p k n", k=MC),
                             W2[e].rearrange("(k p) n -> p k n", p=128)).then_inc(w_in[e], 16)
                sp.dma_start(wraw[:, e, HID + MC * HID:].rearrange("p (k n) -> p k n", k=MC),
                             W3[e].rearrange("(k p) n -> p k n", p=128)).then_inc(w_in[e], 16)

            sp.wait_ge(s.const_zero, 11)
            zeros = zrow[:].unsqueeze(1).to_broadcast([128, PAD // 128, D])
            sp.dma_start(xnd[T:T + PAD, :].rearrange("(c p) d -> p c d", p=128), zeros).then_inc(s.xn_out, 16)
            sp.dma_start(out[T:T + PAD, :].rearrange("(c p) d -> p c d", p=128), zeros).then_inc(s.x2_out, 16)
            for b in range(B):
                sp.wait_ge(s.x2_done, b + 1)
                sp.dma_start(out[b * S:(b + 1) * S, :], x2[:, b, :]).then_inc(s.x2_out, 16)
                sp.wait_ge(s.xn_done, b + 1)
                sp.dma_start(xnd[b * S:(b + 1) * S, :], xn[:, b, :]).then_inc(s.xn_out, 16)

        @block.gpsimd
        def _(pool):
            g = nc.gpsimd
            g.memset(onesb[:], 1.0).then_inc(s.ones_done, 1)
            g.memset(identf[:], 0.0).then_inc(s.const_zero, 1)
            g.memset(minus_half[:], -0.5).then_inc(s.const_zero, 1)
            g.memset(delta[:], 1.0).then_inc(s.const_zero, 1)
            g.memset(wq[:], 0.0).then_inc(s.wq_zero, 1)
            g.memset(wc[:], 0.0).then_inc(s.wq_zero, 1)
            pool.wait_ge(s.const_zero, 3)
            g.affine_select(out=identf[:], in_=identf[:], compare_op=ALU.not_equal, fill=1.0, base=0,
                            pattern=[[-1, 128]], channel_multiplier=1).then_inc(s.const_done, 1)
            g.affine_select(out=delta[:], in_=delta[:], compare_op=ALU.is_ge, fill=0.0, base=0,
                            pattern=[[-3, NH]], channel_multiplier=1).then_inc(s.const_done, 1)
            pool.wait_ge(s.const_done, 2)
            g.affine_select(out=delta[:], in_=delta[:], compare_op=ALU.is_ge, fill=0.0, base=2,
                            pattern=[[3, NH]], channel_multiplier=-1).then_inc(s.delta_done, 1)
            g.memset(hmask[:], 0.25).then_inc(s.const_zero, 1)
            g.memset(onecol[:], 1.0).then_inc(s.const_zero, 1)
            g.memset(ones64[:], 1.0).then_inc(s.const_zero, 1)
            for i in range(2):
                pool.wait_ge(s.ve1_done, i + 1)
                g.tensor_tensor(rs1[:, 4 * i:4 * i + 4], ve1[:, 4 * i:4 * i + 4], minus_half[:, 0:4], ALU.pow)\
                    .then_inc(s.rs1_done, 1)
            g.memset(identb[:], 0.0).then_inc(s.const_zero, 1)
            g.memset(negb[:], NEG).then_inc(s.const_zero, 1)
            pool.wait_ge(s.const_zero, 8)
            g.affine_select(out=hmask[:], in_=hmask[:], compare_op=ALU.is_ge, fill=0.0, base=0,
                            pattern=[[-DH, NH]], channel_multiplier=1).then_inc(s.const_done, 1)
            g.affine_select(out=identb[:], in_=identb[:], compare_op=ALU.not_equal, fill=1.0, base=0,
                            pattern=[[-1, 128]], channel_multiplier=1).then_inc(s.const_done, 1)
            g.affine_select(out=negb[:], in_=negb[:], compare_op=ALU.is_gt, fill=0.0, base=0,
                            pattern=[[-1, 128]], channel_multiplier=1).then_inc(s.const_done, 1)
            pool.wait_ge(s.const_done, 3)
            g.affine_select(out=hmask[:], in_=hmask[:], compare_op=ALU.is_ge, fill=0.0, base=DH - 1,
                            pattern=[[DH, NH]], channel_multiplier=-1).then_inc(s.const_done, 1)
            pool.wait_ge(s.const_done, 6)
            g.memset(LT[:], 1.0).then_inc(s.lt_ones, 1)

            def make_qbd(b):
                if b >= 2:
                    pool.wait_ge(s.qk_ps, 2 * (b - 1))
                g.tensor_tensor(qbd[:, b % 2, :, :], qT[:, b:b + 1, :].to_broadcast([128, NH, S]),
                                hmask[:].unsqueeze(2).to_broadcast([128, NH, S]), ALU.mult).then_inc(s.qbd_done, 1)
            pool.wait_ge(s.qT_done, 1)
            make_qbd(0)
            g.memset(v1[:, :, :, DH:DH + 1], 1.0).then_inc(s.v1_done, 1)
            for i in range(2):
                pool.wait_ge(ctx_in[i], 16)
                g.tensor_copy(v1[:, 4 * i:4 * i + 4, :, 0:DH],
                              cs_in[:, 4 * i:4 * i + 4, :].rearrange("p b (h c) -> p b h c", c=DH)).then_inc(s.v1_done, 1)
                if i == 0:
                    make_qbd(1)
            g.memset(trib[:], 1.0).then_inc(s.const_zero, 1)
            g.memset(zrow[:], 0.0).then_inc(s.const_zero, 1)
            g.memset(prefb[:, 0, :], 0.0).then_inc(s.const_zero, 1)
            pool.wait_ge(s.const_zero, 11)
            g.affine_select(out=trib[:], in_=trib[:], compare_op=ALU.is_gt, fill=0.0, base=0,
                            pattern=[[1, 128]], channel_multiplier=-1).then_inc(s.const_done, 1)
            g.iota(iota[:], pattern=[[1, 128]], base=0, channel_multiplier=0,
                   allow_small_or_imprecise_dtypes=True).then_inc(s.iota_done, 1)
            g.iota(iotab[:], pattern=[[1, 128]], base=0, channel_multiplier=0,
                   allow_small_or_imprecise_dtypes=True).then_inc(s.iota_done, 1)
            g.iota(tokval[:], pattern=[[S, B]], base=-2 * T, channel_multiplier=1,
                   allow_small_or_imprecise_dtypes=True).then_inc(s.iota_done, 1)
            g.iota(padval[:], pattern=[[0, NC // 3], [128, 3]], base=-T, channel_multiplier=1,
                   allow_small_or_imprecise_dtypes=True).then_inc(s.iota_done, 1)
            g.iota(ebase[:], pattern=[[PLACES, NE]], base=0, channel_multiplier=0,
                   allow_small_or_imprecise_dtypes=True).then_inc(s.iota_done, 1)
            def rsqrt(dst, src, wait, done, j):
                pool.wait_ge(wait, j + 1)
                g.tensor_tensor(dst[:, 2 * j:2 * j + 2], src[:, 2 * j:2 * j + 2], minus_half[:, 0:2], ALU.pow)\
                    .then_inc(done, 1)

            def weights_lo(e, layer):
                hi, lo = ((s.whi1_done, s.wlo1_done), None, (s.whi3_done, s.wlo3_done))[layer - 1]
                c = LAYER[layer]
                pool.wait_ge(hi, e + 1)
                g.tensor_tensor(wlo[e % 2][:, c], wraw[:, e, c], whi[e % 2][:, c].bitcast(F32), ALU.subtract).then_inc(lo, 1)

            def rows_onehot(j):
                pool.wait_ge(s.rf_done, j + 1)
                for b in (2 * j, 2 * j + 1):
                    for k in range(2):
                        g.tensor_scalar(ohb[:, 2 * b + k, :], iotab[:], rf[:, b, k:k + 1], None, ALU.is_equal)\
                            .then_inc(s.ohb_pool, 1)

            def chunks_onehot(j):
                for b in (2 * j, 2 * j + 1):
                    for k in range(2):
                        g.tensor_scalar(oha[:, 2 * b + k, :], iotab[:, 0:NC], cf[:, b, k:k + 1], tokval[:, b:b + 1],
                                        ALU.is_equal, ALU.mult).then_inc(s.oha_pool, 1)
            NP = B // 2
            for j in range(NP + 1):
                if j + 1 < NP:
                    make_qbd(2 * j + 2)
                if j >= 1:
                    rsqrt(rs2, ve2, s.ve2_done, s.rs2_done, j - 1)
                if j + 1 < NP:
                    make_qbd(2 * j + 3)
                if j >= 1:
                    rsqrt(rs3, ve3, s.ve3_done, s.rs3_done, j - 1)
                if j >= NP - 1:
                    rows_onehot(j - NP + 1)
                if j == 2:
                    weights_lo(0, 1)
            chunks_onehot(0)
            chunks_onehot(1)
            weights_lo(0, 3)

            def gather(e):
                if e >= 2:
                    pool.wait_ge(s.xT_ps, e - 1)
                for c in range(3):
                    n = min(128, MAIN - 128 * c)
                    col = CHUNKS * e + c
                    g.indirect_dma_start(out=xg[0:n, e % 2, c, :], out_offset=None, in_=xnd,
                                         in_offset=bass.IndirectOffsetOnAxis(ap=ids[0:n, col:col + 1], axis=0))\
                        .then_inc(gathered[e % 2], 16)

            def scatter(e):
                pool.wait_ge(s.ys_done, e + 1)
                if e >= 1:
                    pool.wait_ge(s.added, 48 * e)
                for c in range(3):
                    if e == NE - 1 and c >= 1:
                        pool.wait_ge(s.ys_done, e + 1 + c)
                    n = min(128, MAIN - 128 * c)
                    col = CHUNKS * e + c
                    g.indirect_dma_start(out=out, out_offset=bass.IndirectOffsetOnAxis(ap=ids[0:n, col:col + 1], axis=0),
                                         in_=ys[0:n, e % 2, c, :], in_offset=None, compute_op=ALU.add)\
                        .then_inc(s.added, 16)
            pool.wait_ge(s.ids_done, 1)
            pool.wait_ge(s.xn_out, 16 * (B + 1))
            pool.wait_ge(s.x2_out, 16 * (B + 1))
            gather(0)
            gather(1)
            for e in range(NE):
                if e + 1 < NE:
                    weights_lo(e + 1, 1)
                if e + 2 < NE:
                    gather(e + 2)
                if e + 1 < NE:
                    weights_lo(e + 1, 3)
                if e >= 1:
                    scatter(e - 1)
                if e == 2:
                    most = most_tokens(pool)
            scatter(NE - 1)
            pool.wait_ge(s.added, 48 * NE)

            def tick(before=None):
                if before is not None:
                    pool.wait_ge(s.r_turn, before)
                g.tensor_tensor(turn[:], onecol[:], onecol[:], ALU.mult).then_inc(s.r_turn, 1)

            with pool.If(most > MAIN):
                tick()
                with pool.Fori(0, NE) as e:
                    pool.wait_ge(s.r_whi, e + 1)
                    g.tensor_tensor(wlo[0][:], wraw[:, bass.ds(e, 1), :].rearrange("p o w -> p (o w)"),
                                    whi[0][:].bitcast(F32), ALU.subtract).then_inc(s.r_wlo, 1)
                    for c in range(STEPS):
                        over = STEPS * e + c
                        pool.wait_ge(s.r_ids, over + 1)
                        tick(3 * over + 1)
                        for j in range(RC):
                            g.indirect_dma_start(out=xg[:, 0, j, :], out_offset=None, in_=xnd,
                                                 in_offset=bass.IndirectOffsetOnAxis(ap=rids[:, j:j + 1], axis=0))\
                                .then_inc(s.r_gathered, 16)
                        pool.wait_ge(s.r_ys, over + 1)
                        tick(3 * over + 2)
                        for j in range(RC):
                            g.indirect_dma_start(out=out, out_offset=bass.IndirectOffsetOnAxis(ap=rids[:, j:j + 1], axis=0),
                                                 in_=ys[:, 0, j, :], in_offset=None, compute_op=ALU.add)\
                                .then_inc(s.r_added, 16)
                        pool.wait_ge(s.r_added, 16 * RC * (over + 1))
                        tick(3 * over + 3)

        @block.scalar
        def _(act):
            a = nc.scalar
            a.preload_act_table_set("natural_log_exp_and_others")
            for lo, src in ((0, igw), (24, fgw)):
                act.dma_start(gw[lo:lo + 24, :], src.rearrange("h (c d) -> (h c) d", c=3)).then_inc(s.gw_in, 16)
            for lo, src in ((0, igb), (BH, fgb)):
                act.dma_start(gbias[lo:lo + BH, :], src.rearrange("(o h) -> o h", o=1).to_broadcast([B, NH]))\
                    .then_inc(s.bias_in, 16)
            act.dma_start(lnsb[:], lns.partition_broadcast(128)).then_inc(s.bias_in, 16)
            def select_heads(b):
                a.activation(RH[0:3 * NH, NH * b:NH * b + NH, :], delta[:].unsqueeze(2).to_broadcast([3 * NH, NH, S]),
                             ACT.Copy).then_inc(s.rh_done, 1)
            for src, ready, dst, done in ((bank[6], s.cT_ps, cT, s.cT_done), (bank[7], s.cT_ps, cT, s.cT_done),
                                          (bank[3], s.qT_ps, qT, s.qT_done), (bank[4], s.qT_ps, qT, s.qT_done)):
                i = 0 if src is bank[6] or src is bank[3] else 1
                act.wait_ge(ready, 4 * i + 4)
                a.activation(dst[:, 4 * i:4 * i + 4, :], src[:].rearrange("p (b t) -> p b t", t=S), ACT.Copy).then_inc(done, 1)
            act.wait_ge(s.delta_done, 1)
            for b in range(3):
                select_heads(b)
            act.wait_ge(s.nabs_done, 1)
            a.activation(expn[:], nabs[:], ACT.Exp).then_inc(s.expn_done, 1)
            act.wait_ge(s.expn_done, 1)
            a.activation(nabs[:], expn[:], ACT.Ln, bias=onecol[0:BH, :]).then_inc(s.softplus_done, 1)
            act.wait_ge(s.mld_done, 1)
            a.activation(em[:], mld[:], ACT.Exp, scale=-1.0).then_inc(s.em_done, 1)
            for b in range(3, 5):
                select_heads(b)
            act.wait_ge(s.emT_ps, 1)
            a.activation(emT[:], misc[:, 0:BH], ACT.Copy).then_inc(s.emT_done, 1)

            def weights_hi(e, layer, pieces=range(MC)):
                if layer == 1:
                    act.wait_ge(w_in[e], 48)
                if e >= 2:
                    act.wait_ge((s.l1_ps, s.l2_ps, s.l3_ps)[layer - 1], (1 if layer == 3 else MC) * (e - 1))
                done = (s.whi1_done, s.whi2_done, s.whi3_done)[layer - 1]
                c = LAYER[layer]
                for a_ in [c.start + HID * k for k in (pieces if layer == 2 else (0,))]:
                    a.activation(whi[e % 2][:, a_:a_ + HID], wraw[:, e, a_:a_ + HID], ACT.Copy).then_inc(done, 1)

            def decay(b):
                if b >= 2:
                    act.wait_ge(s.pv_ps, b - 1)
                for half in range(2):
                    act.wait_ge(s.arg_ps, 2 * b + half + 1)
                    a.activation(dec[:, b % 2, half * 4:half * 4 + 4, :],
                                 arg_bank[half][:].rearrange("p (h t) -> p h t", t=S), ACT.Exp).then_inc(s.dec_done, 1)
            NP = B // 2
            for j in range(NP + 2):
                if j < NP:
                    decay(2 * j)
                if j >= 2:
                    act.wait_ge(s.xnT_ps, j - 1)
                    a.activation(xnT[:], xnT_bank(j - 2)[:, 0:2 * S].rearrange("p (i t) -> p i t", t=S), ACT.Copy)\
                        .then_inc(s.xnT_done, 1)
                if j == 0:
                    select_heads(5)
                elif j == 1:
                    weights_hi(0, 1)
                elif j < NP:
                    weights_hi(0, 2, [2 * j - 3])
                if j < B // 2:
                    decay(2 * j + 1)
                if j == 0:
                    select_heads(6)
                elif j == 3:
                    weights_hi(0, 3)
                elif j < NP:
                    weights_hi(0, 2, [2 * j - 2])
                if j == 1:
                    select_heads(7)
            a.preload_act_table(ACT.Gelu)

            def gelu(e, layer, ms=range(MC)):
                psd, done, split, dst, col = ((s.l1_ps, s.gelu1_done, s.g1l_done, g1, 0),
                                              (s.l2_ps, s.gelu2_done, s.g2l_done, g2, 32))[layer - 1]
                for m in ms:
                    act.wait_ge(psd, MC * e + m + 1)
                    if e >= 1:
                        act.wait_ge(split, MC * (e - 1) + m + 1)
                    a.activation(dst[:, m, :], bank[m][:, 0:MAIN], ACT.Gelu,
                                 bias=smt[:, col + MC * e + m:col + MC * e + m + 1]).then_inc(done, 1)

            def scale_y(e):
                act.wait_ge(s.l3_ps, e + 1)
                if e == 0:
                    act.wait_ge(s.b3h_done, 1)
                if e >= 1:
                    act.wait_ge(s.y_ps, e)
                if e == NE - 1:
                    for c in range(3):
                        cols = slice(128 * c, min(128 * c + 128, MAIN))
                        a.activation(yT[:, cols], bank[4][:, cols], ACT.Identity, bias=b3h[:, e:e + 1], scale=0.5)\
                            .then_inc(s.yT_done, 1)
                    return
                a.activation(yT[:], bank[4][:, 0:MAIN], ACT.Identity, bias=b3h[:, e:e + 1], scale=0.5)\
                    .then_inc(s.yT_done, 1)
            act.wait_ge(s.ids_done, 1)
            act.wait_ge(s.xn_out, 16 * (B + 1))
            act.wait_ge(s.x2_out, 16 * (B + 1))
            gelu(0, 1)
            for e in range(NE):
                if e + 1 < NE:
                    weights_hi(e + 1, 1)
                if e >= 1:
                    scale_y(e - 1)
                if e + 1 < NE:
                    weights_hi(e + 1, 2)
                gelu(e, 2, range(0, 1))
                if e + 1 < NE:
                    weights_hi(e + 1, 3)
                gelu(e, 2, range(1, MC))
                if e + 1 < NE:
                    gelu(e + 1, 1)
                if e == 2:
                    most = most_tokens(act)
            scale_y(NE - 1)

            with act.If(most > MAIN):
                with act.Fori(0, NE) as e:
                    act.wait_ge(s.r_turn, 3 * STEPS * e + 1)
                    a.activation(whi[0][:], wraw[:, bass.ds(e, 1), :].rearrange("p o w -> p (o w)"), ACT.Copy)\
                        .then_inc(s.r_whi, 1)
                    for c in range(STEPS):
                        for psd, done, dst, col in ((s.r_l1, s.r_gelu1, g1, 0), (s.r_l2, s.r_gelu2, g2, MC)):
                            act.wait_ge(psd, STEPS * e + c + 1)
                            for m in range(MC):
                                a.activation(dst[:, m, 0:REST], bank[m][:, 0:REST], ACT.Gelu,
                                             bias=rbias[:, col + m:col + m + 1]).then_inc(done, 1)

        @block.vector
        def _(dve):
            v = nc.vector
            for i in range(2):
                dve.wait_ge(x_in[i], 16)
                for b in range(4 * i, 4 * i + 4):
                    v.bn_stats(st1[:, b, :], xs[:, b, :]).then_inc(s.st1_done, 1)
                for b in range(4 * i, 4 * i + 4):
                    dve.wait_ge(s.st1_done, b + 1)
                    v.bn_aggr(mv1[:, b, :], st1[:, b, :]).then_inc(s.mv1_done, 1)
                dve.wait_ge(s.mv1_done, 4 * i + 4)
                v.tensor_scalar_add(ve1[:, 4 * i:4 * i + 4], mv1[:, 4 * i:4 * i + 4, 1], EPS_LN).then_inc(s.ve1_done, 1)
            dve.wait_ge(s.gw_T, 1)
            v.tensor_copy(gwt[:], bank[1][:, 0:48]).then_inc(s.gwt_done, 1)
            dve.wait_ge(s.gwt_done, 1)
            dve.wait_ge(s.wq_zero, 2)
            pad = BH * 2 + NH

            def padded(w):
                return w[:].rearrange("p (b c) -> p b c", c=pad)[:, :, 0:2 * BH]\
                    .rearrange("p b (g c) -> p b g c", c=BH)[:, :, :, 0:NH]

            def gate_part(c):
                return gwt[:].rearrange("p (g h c) -> p g h c", g=2, c=3)[:, :, :, c]\
                    .unsqueeze(1).to_broadcast([128, B, 2, NH])
            for gg in range(2):
                v.tensor_copy(padded(wq)[:, :, gg, :], gate_part(0)[:, :, gg, :]).then_inc(s.wpad_done, 1)
                v.tensor_tensor(padded(wc)[:, :, gg, :], gate_part(1)[:, :, gg, :], gate_part(2)[:, :, gg, :],
                                ALU.add).then_inc(s.wpad_done, 1)
            for b in range(B):
                if b % 4 == 0:
                    dve.wait_ge(s.rs1_done, b // 4 + 1)
                v.tensor_scalar(qn[:, b, :], xs[:, b, :], mv1[:, b, 0:1], rs1[:, b:b + 1], ALU.subtract, ALU.mult)\
                    .then_inc(s.qn_done, 1)
            dve.wait_ge(s.gates_ps, 1)
            dve.wait_ge(s.bias_in, 48)
            v.tensor_scalar(fgt[:], pv_bank[0][BH:128, 0:S], gbias[BH:128, :], None, ALU.add).then_inc(s.fgt_done, 1)
            dve.wait_ge(s.fgt_done, 1)
            v.scalar_tensor_tensor(out=nabs[:], in0=fgt[:], scalar=-1.0, in1=fgt[:], op0=ALU.mult, op1=ALU.min)\
                .then_inc(s.nabs_done, 1)
            dve.wait_ge(s.sm_T, 1)
            v.tensor_copy(smt[:], misc[:, 128:208]).then_inc(s.smt_done, 1)
            dve.wait_ge(s.smt_done, 1)
            v.tensor_scalar(b3h[:], smt[:, 64:72], 0.5, None, ALU.mult).then_inc(s.b3h_done, 1)
            dve.wait_ge(s.softplus_done, 1)
            v.scalar_tensor_tensor(out=logf[:], in0=fgt[:], scalar=0.0, in1=nabs[:], op0=ALU.min, op1=ALU.subtract)\
                .then_inc(s.logf_done, 1)
            dve.wait_ge(s.logf_done, 1)
            dve.wait_ge(s.const_zero, 6)
            v.tensor_tensor_scan(lsum[:], ones64[:], logf[:], 0.0, ALU.mult, ALU.add).then_inc(s.lsum_done, 1)
            dve.wait_ge(s.lsum_done, 1)
            v.scalar_tensor_tensor(out=um[0:BH, :], in0=pv_bank[0][0:BH, 0:S], scalar=gbias[0:BH, :], in1=lsum[:],
                                   op0=ALU.add, op1=ALU.subtract).then_inc(s.u_done, 1)
            dve.wait_ge(s.u_done, 1)
            v.tensor_tensor_scan(cm[:], um[0:BH, :], um[0:BH, :], -3e38, ALU.max, ALU.max).then_inc(s.cm_done, 1)
            dve.wait_ge(s.cm_done, 1)
            v.tensor_scalar(um[BH:128, :], cm[:], -1.0, None, ALU.mult).then_inc(s.um_done, 1)
            v.tensor_tensor(mld[:], cm[:], lsum[:], ALU.add).then_inc(s.mld_done, 1)
            dve.wait_ge(s.um_done, 1)
            v.tensor_copy(parts[:, 0, :], um[:]).then_inc(s.part_done, 1)
            dve.wait_ge(s.part_done, 1)
            v.tensor_tensor(um1[:], um[:], parts[:, 0, :], ALU.subtract).then_inc(s.um1_done, 1)
            dve.wait_ge(s.um1_done, 1)
            v.tensor_copy(parts[:, 1, :], um1[:]).then_inc(s.part_done, 1)
            dve.wait_ge(s.part_done, 2)
            v.tensor_tensor(parts[:, 2, :], um1[:], parts[:, 1, :], ALU.subtract).then_inc(s.part_done, 1)
            dve.wait_ge(s.emT_done, 1)
            v.tensor_scalar_add(emTe[:], emT[:], EPS_NORMALIZER).then_inc(s.emTe_done, 1)
            dve.wait_ge(s.iota_done, 5)
            dve.wait_ge(s.emTe_done, 1)

            def weigh(b):
                for half in range(2):
                    dve.wait_ge(s.dec_done, 2 * b + half + 1)
                    dve.wait_ge(s.qk_ps, 2 * b + half + 1)
                    v.tensor_tensor(cw[:, b % 2, half * 4:half * 4 + 4, :],
                                    qk_bank(b, half)[:].rearrange("p (h t) -> p h t", t=S),
                                    dec[:, b % 2, half * 4:half * 4 + 4, :], ALU.mult).then_inc(s.cw_done, 1)

            def normalise_and_route(j, r):
                norm = 0 <= j < NP
                route = 0 <= r < NP
                p = j % 2
                if norm:
                    pv = pv_bank[p][:, 0:2 * NH * (DH + 1)].rearrange("p (i h c) -> p i h c", i=2, c=DH + 1)
                    floor = emTe[:, 2 * NH * j:2 * NH * (j + 1)].rearrange("p (i h) -> p i h", h=NH)
                    dve.wait_ge(s.pv_ps, 2 * j + 2)
                    v.scalar_tensor_tensor(out=den1[:, p, :, :], in0=pv[:, :, :, DH], scalar=EPS_NORMALIZER, in1=floor,
                                           op0=ALU.add, op1=ALU.max).then_inc(s.den1_done, 1)
                    v.tensor_scalar(den2[:, p, :, :], pv[:, :, :, DH], -1.0, EPS_NORMALIZER, ALU.mult, ALU.add)\
                        .then_inc(s.den2_done, 1)
                if route:
                    pair = slice(2 * r, 2 * r + 2)
                    rk = misc[:, 288:288 + 2 * NE].rearrange("p (i e) -> p i e", e=NE)
                    dve.wait_ge(s.rank_ps, r + 1)
                    v.tensor_scalar(beyond[:], rk, float(MAIN), float(GAP), ALU.is_ge, ALU.mult).then_inc(s.beyond_done, 1)
                if norm:
                    dve.wait_ge(s.den1_done, j + 1)
                    dve.wait_ge(s.den2_done, j + 1)
                    v.tensor_tensor(den[:, p, :, :], den1[:, p, :, :], den2[:, p, :, :], ALU.max).then_inc(s.den_done, 1)
                if route:
                    dve.wait_ge(s.beyond_done, r + 1)
                    v.tensor_tensor(beyond[:], beyond[:], rk, ALU.add).then_inc(s.place_done, 1)
                if norm:
                    dve.wait_ge(s.den_done, j + 1)
                    v.reciprocal(rden[:, p, :, :], den[:, p, :, :]).then_inc(s.rden_done, 1)
                if route:
                    dve.wait_ge(s.place_done, r + 1)
                    v.tensor_tensor(place[:], beyond[:], ebase[:].unsqueeze(1).to_broadcast([128, 2, NE]), ALU.add)\
                        .then_inc(s.base_done, 1)
                if norm:
                    dve.wait_ge(s.rden_done, j + 1)
                    v.tensor_tensor(hn[:, p, :, :].rearrange("p i (h c) -> p (i h) c", c=DH),
                                    pv.rearrange("p i h c -> p (i h) c")[:, :, 0:DH],
                                    rden[:, p, :, :].rearrange("p i h -> p (i h)").unsqueeze(2)
                                    .to_broadcast([128, 2 * NH, DH]), ALU.mult).then_inc(s.hn_done, 1)
                if route:
                    dve.wait_ge(s.base_done, r + 1)
                    v.tensor_tensor(placed[:], ohk[:, pair, :, :], place[:].unsqueeze(2).to_broadcast([128, 2, 2, NE]),
                                    ALU.mult).then_inc(s.placed_done, 1)
                if norm:
                    dve.wait_ge(s.hn_done, j + 1)
                    for i in range(2):
                        v.bn_stats(st2[:, p, i, :], hn[:, p, i, :]).then_inc(s.st2_done, 1)
                if route:
                    dve.wait_ge(s.placed_done, r + 1)
                    v.tensor_reduce(sl[:, pair, :], placed[:], axis=AX.X, op=ALU.add).then_inc(s.sl_done, 1)
                if norm:
                    for i in range(2):
                        dve.wait_ge(s.st2_done, 2 * j + i + 1)
                        v.bn_aggr(mv2[:, 2 * j + i, :], st2[:, p, i, :]).then_inc(s.mv2_done, 1)
                if route:
                    dve.wait_ge(s.sl_done, r + 1)
                    v.tensor_scalar(slf[:, pair, :], sl[:, pair, :], 1.0 / 128, -63.5 / 128, ALU.mult, ALU.add)\
                        .then_inc(s.slf_done, 1)
                if norm:
                    dve.wait_ge(s.mv2_done, 2 * j + 2)
                    v.tensor_scalar_add(ve2[:, 2 * j:2 * j + 2], mv2[:, 2 * j:2 * j + 2, 1], EPS_LN).then_inc(s.ve2_done, 1)
                if route:
                    dve.wait_ge(s.slf_done, r + 1)
                    v.tensor_scalar(cf[:, pair, :], slf[:, pair, :], ROUND, -ROUND, ALU.add, ALU.add)\
                        .then_inc(s.cf_done, 1)
                if norm:
                    for i in range(2):
                        v.scalar_tensor_tensor(out=hl[:, p, i, :], in0=hn[:, p, i, :], scalar=mv2[:, 2 * j + i, 0:1],
                                               in1=lnsb[:], op0=ALU.subtract, op1=ALU.mult).then_inc(s.hl_done, 1)
                if route:
                    dve.wait_ge(s.cf_done, r + 1)
                    v.scalar_tensor_tensor(out=rf[:, pair, :], in0=cf[:, pair, :], scalar=-128.0, in1=sl[:, pair, :],
                                           op0=ALU.mult, op1=ALU.add).then_inc(s.rf_done, 1)

            def onehots(b):
                dve.wait_ge(s.rf_done, b // 2 + 1)
                for k in range(2):
                    v.tensor_scalar(ohb[:, 2 * b + k, :], iotab[:], rf[:, b, k:k + 1], None, ALU.is_equal)\
                        .then_inc(s.onehots_dve, 1)
                    v.tensor_scalar(oha[:, 2 * b + k, :], iotab[:, 0:NC], cf[:, b, k:k + 1], tokval[:, b:b + 1],
                                    ALU.is_equal, ALU.mult).then_inc(s.onehots_dve, 1)

            def residual_and_choose(j, c):
                res = 0 <= j < NP
                choose = 0 <= c < NP
                p = j % 2
                if res:
                    dve.wait_ge(s.rs2_done, j + 1)
                    dve.wait_ge(s.hl_done, 2 * j + 2)
                    for i in range(2):
                        b = 2 * j + i
                        v.scalar_tensor_tensor(out=x2[:, b, :], in0=hl[:, p, i, :], scalar=rs2[:, b:b + 1],
                                               in1=xs[:, b, :], op0=ALU.mult, op1=ALU.add).then_inc(s.x2_done, 1)
                if choose:
                    pair = slice(2 * c, 2 * c + 2)
                    dve.wait_ge(s.score_ps, c + 1)
                    for i in range(2):
                        v.max(top[:, 2 * c + i, :], score_bank(c)[:, 256 + 8 * i:264 + 8 * i]).then_inc(s.top_done, 1)
                if res:
                    for i in range(2):
                        dve.wait_ge(s.x2_done, 2 * j + i + 1)
                        v.bn_stats(st3[:, p, i, :], x2[:, 2 * j + i, :]).then_inc(s.st3_done, 1)
                if choose:
                    for i in range(2):
                        dve.wait_ge(s.top_done, 2 * c + i + 1)
                        v.max_index(topi[:, 2 * c + i, :], top[:, 2 * c + i, :], score_bank(c)[:, 256 + 8 * i:264 + 8 * i])\
                            .then_inc(s.topi_done, 1)
                if res:
                    for i in range(2):
                        dve.wait_ge(s.st3_done, 2 * j + i + 1)
                        v.bn_aggr(mv3[:, 2 * j + i, :], st3[:, p, i, :]).then_inc(s.mv3_done, 1)
                if choose:
                    dve.wait_ge(s.topi_done, 2 * c + 2)
                    v.tensor_copy(topf[:, pair, :], topi[:, pair, 0:2]).then_inc(s.topf_done, 1)
                if res:
                    dve.wait_ge(s.mv3_done, 2 * j + 2)
                    v.tensor_scalar_add(ve3[:, 2 * j:2 * j + 2], mv3[:, 2 * j:2 * j + 2, 1], EPS_LN).then_inc(s.ve3_done, 1)
                if choose:
                    dve.wait_ge(s.topf_done, c + 1)
                    v.tensor_tensor(ohk[:, pair, :, :].rearrange("p b k e -> p (b k) e"),
                                    iota[:, 0:NE].unsqueeze(1).to_broadcast([128, 4, NE]),
                                    topf[:, pair, :].rearrange("p b k -> p (b k)").unsqueeze(2).to_broadcast([128, 4, NE]),
                                    ALU.is_equal).then_inc(s.oh_done, 1)
                    dve.wait_ge(s.oh_done, c + 1)
                    v.tensor_tensor(maskb[:, pair, :], ohk[:, pair, 0, :], ohk[:, pair, 1, :], ALU.add)\
                        .then_inc(s.mask_done, 1)
                    dve.wait_ge(s.mask_done, c + 1)
                    for b in (2 * c, 2 * c + 1):
                        if b >= 1:
                            dve.wait_ge(s.pref_done, b)
                        v.tensor_tensor(prefb[:, b + 1, :], prefb[:, b, :], maskb[:, b, :], ALU.add).then_inc(s.pref_done, 1)

            def norm2(j):
                dve.wait_ge(s.rs3_done, j + 1)
                for b in (2 * j, 2 * j + 1):
                    v.tensor_scalar(xn[:, b, :], x2[:, b, :], mv3[:, b, 0:1], rs3[:, b:b + 1], ALU.subtract, ALU.mult)\
                        .then_inc(s.xn_done, 1)

            NP = B // 2
            for j in range(NP):
                weigh(2 * j)
                if j >= 1:
                    normalise_and_route(j - 1, j - 3)
                weigh(2 * j + 1)
                if j >= 1:
                    residual_and_choose(j - 1, j - 2)
                    norm2(j - 1)
            normalise_and_route(NP - 1, NP - 3)
            residual_and_choose(NP - 1, NP - 2)
            norm2(NP - 1)
            normalise_and_route(-1, NP - 2)
            onehots(B - 4)
            residual_and_choose(-1, NP - 1)
            onehots(B - 3)
            dve.wait_ge(s.rank_ps, NP)
            v.tensor_reduce(cntf[:], misc[:, 320:320 + NE], axis=AX.X, op=ALU.max).then_inc(s.cnt_done, 1)
            normalise_and_route(-1, NP - 1)
            onehots(B - 2)
            onehots(B - 1)
            dve.wait_ge(s.cnt_done, 1)
            v.tensor_copy(cnti[:], cntf[:]).then_inc(s.cnti_done, 1)
            lists = lists_bank[:, 0:NC]
            dve.wait_ge(s.lists_ps, 1)
            v.scalar_tensor_tensor(out=padterm[:], in0=lists, scalar=0.0, in1=padval[:].rearrange("p a c -> p (a c)"),
                                   op0=ALU.is_equal, op1=ALU.mult).then_inc(s.padterm_done, 1)
            dve.wait_ge(s.padterm_done, 1)
            v.scalar_tensor_tensor(out=ids[:], in0=lists, scalar=float(2 * T), in1=padterm[:], op0=ALU.add, op1=ALU.add)\
                .then_inc(s.ids_done, 1)

            def split_x(e):
                dve.wait_ge(s.xT_ps, e + 1)
                if e >= 1:
                    dve.wait_ge(s.l1_ps, MC * e)
                v.tensor_copy(xhi[:], bank[5][:, 0:MAIN]).then_inc(s.xhi_done, 1)
                dve.wait_ge(s.xhi_done, e + 1)
                v.tensor_tensor(xlo[:], bank[5][:, 0:MAIN], xhi[:].bitcast(F32), ALU.subtract).then_inc(s.xlo_done, 1)

            def split_g(e, layer, ms=range(MC)):
                gd, hd, ld, g, gh, gl = ((s.gelu1_done, s.g1h_done, s.g1l_done, g1, g1h, g1l),
                                         (s.gelu2_done, s.g2h_done, s.g2l_done, g2, g2h, g2l))[layer - 1]

                def low(m):
                    dve.wait_ge(hd, MC * e + m + 1)
                    v.tensor_tensor(gl[:, m, :], g[:, m, :], gh[:, m, :].bitcast(F32), ALU.subtract).then_inc(ld, 1)
                for m in ms:
                    dve.wait_ge(gd, MC * e + m + 1)
                    v.tensor_copy(gh[:, m, :], g[:, m, :]).then_inc(hd, 1)
                    if m > ms[0]:
                        low(m - 1)
                low(ms[-1])

            def weights_lo2(e, ks=range(MC)):
                for k in ks:
                    dve.wait_ge(s.whi2_done, MC * e + k + 1)
                    c = slice(HID + k * HID, HID + (k + 1) * HID)
                    v.tensor_tensor(wlo[e % 2][:, c], wraw[:, e, c], whi[e % 2][:, c].bitcast(F32), ALU.subtract)\
                        .then_inc(s.wlo2_done, 1)

            def rows_y(e):
                if e >= 2:
                    dve.wait_ge(s.added, 48 * (e - 1))
                if e == NE - 1:
                    for c in range(3):
                        dve.wait_ge(s.y_ps, e + 1 + c)
                        v.tensor_copy(ys[:, e % 2, c, :], y_bank(e, c)[:, 128 * c:128 * c + D]).then_inc(s.ys_done, 1)
                    return
                dve.wait_ge(s.y_ps, e + 1)
                v.tensor_copy(ys[:, e % 2, :, :], bank[6][:, 0:384].rearrange("p (c d) -> p c d", d=D)).then_inc(s.ys_done, 1)
            weights_lo2(0)
            split_x(0)
            split_g(0, 1)
            for e in range(NE):
                more = e + 1 < NE
                if more:
                    weights_lo2(e + 1, range(0, 3))
                split_g(e, 2, range(0, 1))
                if more:
                    split_x(e + 1)
                split_g(e, 2, range(1, 2))
                if e >= 1:
                    rows_y(e - 1)
                if more:
                    weights_lo2(e + 1, range(3, 4))
                split_g(e, 2, range(2, 3))
                split_g(e, 2, range(3, 4))
                if more:
                    split_g(e + 1, 1)
                if e == 2:
                    most = most_tokens(dve)
            rows_y(NE - 1)

            with dve.If(most > MAIN):
                with dve.Fori(0, NE) as e:
                    for c in range(STEPS):
                        n = STEPS * e + c + 1
                        dve.wait_ge(s.r_turn, 3 * n - 2)
                        v.memset(turnd[:], 0.0)
                        v.tensor_copy(rbias[:, 0:MC], smt[:, bass.ds(MC * e, MC)])
                        v.tensor_copy(rbias[:, MC:2 * MC], smt[:, bass.ds(NE * MC + MC * e, MC)])
                        v.tensor_copy(rbias[:, 2 * MC:2 * MC + 1], smt[:, bass.ds(2 * NE * MC + e, 1)]).then_inc(s.r_bias, 1)
                        v.tensor_copy(rids[:], ids[:, bass.ds(CHUNKS * e + 3 + RC * c, RC)]).then_inc(s.r_ids, 1)
                        dve.wait_ge(s.r_xT, n)
                        v.tensor_copy(xhi[:, 0:REST], bank[5][:, 0:REST]).then_inc(s.r_xhi, 1)
                        dve.wait_ge(s.r_xhi, n)
                        v.tensor_tensor(xlo[:, 0:REST], bank[5][:, 0:REST], xhi[:, 0:REST].bitcast(F32), ALU.subtract)\
                            .then_inc(s.r_xlo, 1)
                        for gd, hd, ld, gt, gh, gl in ((s.r_gelu1, s.r_g1h, s.r_g1l, g1, g1h, g1l),
                                                       (s.r_gelu2, s.r_g2h, s.r_g2l, g2, g2h, g2l)):
                            dve.wait_ge(gd, MC * n)
                            v.tensor_copy(gh[:, :, 0:REST], gt[:, :, 0:REST]).then_inc(hd, 1)
                            dve.wait_ge(hd, n)
                            v.tensor_tensor(gl[:, :, 0:REST], gt[:, :, 0:REST], gh[:, :, 0:REST].bitcast(F32),
                                            ALU.subtract).then_inc(ld, 1)
                        dve.wait_ge(s.r_l3, n)
                        dve.wait_ge(s.r_bias, n)
                        v.tensor_scalar(yT[:, 0:REST], bank[4][:, 0:REST], rbias[:, 2 * MC:2 * MC + 1], 0.5,
                                        ALU.add, ALU.mult).then_inc(s.r_yT, 1)
                        dve.wait_ge(s.r_y, n)
                        v.tensor_copy(ys[:, 0, 0:RC, :], bank[6][:, 0:REST].rearrange("p (c d) -> p c d", d=D))\
                            .then_inc(s.r_ys, 1)

        @block.tensor
        def _(pe):
            t = nc.tensor

            def keep_warm(n, scratch=bank[2]):
                for _ in range(n):
                    t.matmul(scratch[:], onesb[:], onesb[:].unsqueeze(1).to_broadcast([128, 4, 128]), start=True, stop=True)
            pe.wait_ge(s.ones_done, 1)
            keep_warm(WARM["inputs"])
            pe.wait_ge(s.const_done, 1)
            for b in range(B):
                if b == 4:
                    pe.wait_ge(s.gw_in, 32)
                    t.transpose(bank[1][:, 0:48], gw[:], identf[0:48, 0:48]).then_inc(s.gw_T, 1)
                    keep_warm(WARM["gate weights"])
                pe.wait_ge(ctx_in[b // 4], 16)
                t.transpose(bank[6 + b // 4][:, (b % 4) * S:(b % 4 + 1) * S], cs_in[:, b, :], identf[:]).then_inc(s.cT_ps, 1)
            def gate_logits(w, src, b):
                return t.matmul(pv_bank[0][:, 0:S], w[:, 2 * BH * b:2 * BH * (b + 1)], src[:, b, :],
                                start=(w is wc and b == 0), stop=(w is wq and b == B - 1))
            for i in range(2):
                for b in range(4 * i, 4 * i + 4):
                    pe.wait_ge(s.qn_done, b + 1)
                    t.transpose(arg_bank[i][:, (b % 4) * S:(b % 4 + 1) * S], qn[:, b, :], identf[:]).then_inc(s.qT_ps, 1)
                if i == 0:
                    pe.wait_ge(s.wpad_done, 4)
                pe.wait_ge(s.cT_done, i + 1)
                for b in range(4 * i, 4 * i + 4):
                    gate_logits(wc, cT, b)
            for b in range(B):
                if b % 4 == 0:
                    pe.wait_ge(s.qT_done, b // 4 + 1)
                last = gate_logits(wq, qT, b)
            last.then_inc(s.gates_ps, 1)
            pe.wait_ge(s.small_in, 16 * 4)
            t.transpose(misc[:, 128:208], sm[:], identf[0:80, 0:80]).then_inc(s.sm_T, 1)

            def logits(b):
                pe.wait_ge(s.qbd_done, b + 1)
                for half in range(2):
                    if 2 * b + half >= 3:
                        pe.wait_ge(s.cw_done, 2 * b + half - 2)
                    t.matmul(qk_bank(b, half)[:], cT[:, b, :],
                             qbd[:, b % 2, half * 4:half * 4 + 4, :].rearrange("p h t -> p (h t)"),
                             start=True, stop=True).then_inc(s.qk_ps, 1)

            def exponents(b):
                if b == 0:
                    pe.wait_ge(s.max_in, 16 * 3)
                    pe.wait_ge(s.lt0_in, 16)
                    pe.wait_ge(s.const_done, 6)
                if b == 1:
                    pe.wait_ge(s.lt1_in, 16)
                if b == 2:
                    pe.wait_ge(s.lt_in, 16 * (B - 2))
                pe.wait_ge(s.rh_done, b + 1)
                for half in range(2):
                    if b >= 1:
                        pe.wait_ge(s.dec_done, 2 * b + half - 1)
                    dst = arg_bank[half][:].rearrange("p (h t) -> p h t", t=S)
                    t.matmul(dst, LT[:, b, :], RH[:, NH * b + 4 * half:NH * b + 4 * half + 4, :], start=True, stop=False)
                    t.matmul(dst, identb[:], negb[:].unsqueeze(1).to_broadcast([128, 4, S]), start=False, stop=True)\
                        .then_inc(s.arg_ps, 1)

            def values(b):
                if b % 2 == 0 and b >= 4:
                    pe.wait_ge(s.hn_done, b // 2 - 1)
                if b % 4 == 0:
                    pe.wait_ge(s.v1_done, b // 4 + 2)
                for h in range(NH):
                    pe.wait_ge(s.cw_done, 2 * b + h // 4 + 1)
                    c = (DH + 1) * (NH * (b % 2) + h)
                    last = t.matmul(pv_bank[b // 2 % 2][:, c:c + DH + 1], cw[:, b % 2, h, :], v1[:, b, h, :],
                                    start=True, stop=True)
                last.then_inc(s.pv_ps, 1)

            def xn_transpose(j):
                pe.wait_ge(s.xn_done, 2 * j + 2)
                if j == 0:
                    pe.wait_ge(s.emT_done, 1)
                elif j < NP - 2:
                    pe.wait_ge(s.topi_done, 2 * j)
                for i in range(2):
                    last = t.transpose(xnT_bank(j)[:, i * S:(i + 1) * S], xn[:, 2 * j + i, :], identf[:])
                last.then_inc(s.xnT_ps, 1)

            def scores(j):
                pe.wait_ge(s.xnT_done, j + 1)
                if 1 <= j < NP - 2:
                    pe.wait_ge(s.place_done, j)
                for i in range(2):
                    last = t.matmul(score_bank(j)[:, 256 + 8 * i:264 + 8 * i], xnT[:, i, :], smt[:, 72:80], start=True, stop=True)
                last.then_inc(s.score_ps, 1)

            def ranks(j):
                pe.wait_ge(s.pref_done, 2 * j + 2)
                if j == 0:
                    pe.wait_ge(s.const_done, 7)
                if j < NP - 3:
                    pe.wait_ge(s.xnT_done, j + 2)
                pair = slice(2 * j, 2 * j + 2)
                t.matmul(misc[:, 288:288 + 2 * NE], trib[:], maskb[:, pair, :].rearrange("p b e -> p (b e)"),
                         start=True, stop=False)
                last = t.matmul(misc[:, 288:288 + 2 * NE], onesb[:], prefb[:, pair, :].rearrange("p b e -> p (b e)"),
                                start=False, stop=True)
                if j == B // 2 - 1:
                    last = t.matmul(misc[:, 320:320 + NE], onesb[:], prefb[:, B, :], start=True, stop=True)
                last.then_inc(s.rank_ps, 1)

            def lists(j):
                for i in range(4):
                    n = 4 * j + i
                    if j < 2:
                        pe.wait_ge(s.oha_pool, n + 1)
                    else:
                        pe.wait_ge(s.onehots_dve, 2 * (n - 8) + 2)
                    last = t.matmul(lists_bank[:, 0:NC], ohb[:, n, :], oha[:, n, :],
                                    start=(n == 0), stop=(n == 2 * B - 1))
                if j == B // 2 - 1:
                    last.then_inc(s.lists_ps, 1)
            NP = B // 2
            for j in range(NP):
                logits(2 * j)
                if j == 0:
                    keep_warm(WARM["gate scans"])
                    pe.wait_ge(s.em_done, 1)
                    pe.wait_ge(s.smt_done, 1)
                    t.transpose(misc[:, 0:BH], em[:], identf[0:BH, 0:BH]).then_inc(s.emT_ps, 1)
                    keep_warm(WARM["gate rows"])
                exponents(2 * j)
                if j >= 2:
                    xn_transpose(j - 2)
                if j >= 1:
                    values(2 * j - 1)
                if j >= 3:
                    ranks(j - 3)
                logits(2 * j + 1)
                exponents(2 * j + 1)
                if j >= 2:
                    scores(j - 2)
                values(2 * j)
            values(B - 1)
            ranks(NP - 3)
            xn_transpose(NP - 2)
            scores(NP - 2)
            keep_warm(WARM["last choice"], bank[3])
            ranks(NP - 2)
            xn_transpose(NP - 1)
            scores(NP - 1)
            ranks(NP - 1)
            for j in range(NP):
                lists(j)

            def x_transpose(e):
                pe.wait_ge(gathered[e % 2], 48 * (e // 2 + 1))
                if e >= 1:
                    pe.wait_ge(s.xlo_done, e)
                for c in range(3):
                    n = min(128, MAIN - 128 * c)
                    last = t.transpose(bank[5][:, 128 * c:128 * c + n], xg[0:n, e % 2, c, :], identf[0:n, 0:n])
                last.then_inc(s.xT_ps, 1)

            def product(dst, e, layer, m, ks, ahi, alo, ready=None):
                p = e % 2
                n = 0
                for k in range(ks):
                    if ready is not None:
                        ready(k)
                    for w, act_ in ((whi, ahi), (wlo, ahi), (whi, alo)):
                        last = t.matmul(dst, wcol(w, p, layer, k, m), act_(k), start=(n == 0), stop=(n == 3 * ks - 1))
                        n += 1
                return last

            def layer1(e):
                pe.wait_ge(s.xlo_done, e + 1)
                pe.wait_ge(s.wlo1_done, e + 1)
                for m in range(MC):
                    if e >= 1:
                        pe.wait_ge(s.gelu2_done, MC * (e - 1) + m + 1)
                    product(bank[m][:, 0:MAIN], e, 1, m, 1, lambda k: xhi[:], lambda k: xlo[:]).then_inc(s.l1_ps, 1)

            def layer2(e):
                def ready(k):
                    pe.wait_ge(s.wlo2_done, MC * e + k + 1)
                    pe.wait_ge(s.g1l_done, MC * e + k + 1)
                for m in range(MC):
                    product(bank[m][:, 0:MAIN], e, 2, m, MC, lambda k: g1h[:, k, :], lambda k: g1l[:, k, :],
                            ready if m == 0 else None).then_inc(s.l2_ps, 1)
                    if m == 0 and e + 1 < NE:
                        x_transpose(e + 1)
                    if m == 0 and e >= 1:
                        y_transpose(e - 1)

            def layer3(e):
                def ready(k):
                    pe.wait_ge(s.g2l_done, MC * e + k + 1)
                pe.wait_ge(s.wlo3_done, e + 1)
                if e >= 1:
                    pe.wait_ge(s.yT_done, e)
                product(bank[4][:, 0:MAIN], e, 3, 0, MC, lambda k: g2h[:, k, :], lambda k: g2l[:, k, :], ready)\
                    .then_inc(s.l3_ps, 1)

            def y_transpose(e):
                pe.wait_ge(s.yT_done, e + 1)
                if e >= 1:
                    pe.wait_ge(s.ys_done, e)
                for c in range(3):
                    if e == NE - 1:
                        pe.wait_ge(s.yT_done, e + 1 + c)
                    n = min(128, MAIN - 128 * c)
                    last = t.transpose(y_bank(e, c)[0:n, 128 * c:128 * c + D], yT[:, 128 * c:128 * c + n], identf[:])
                    if c == 2 or e == NE - 1:
                        last.then_inc(s.y_ps, 1)
            keep_warm(WARM["token lists"], bank[3])
            x_transpose(0)
            keep_warm(WARM["first split"], bank[7])
            layer1(0)
            for e in range(NE):
                layer2(e)
                if e + 1 < NE:
                    layer1(e + 1)
                layer3(e)
                if e == 2:
                    most = most_tokens(pe)
            y_transpose(NE - 1)

            with pe.If(most > MAIN):
                with pe.Fori(0, NE) as e:
                    for c in range(STEPS):
                        n = STEPS * e + c + 1
                        pe.wait_ge(s.r_gathered, 16 * RC * n)
                        for j in range(RC):
                            last = t.transpose(bank[5][:, 128 * j:128 * j + 128], xg[:, 0, j, :], identf[:])
                        last.then_inc(s.r_xT, 1)
                        pe.wait_ge(s.r_xlo, n)
                        if c == 0:
                            pe.wait_ge(s.r_wlo, e + 1)
                        for m in range(MC):
                            last = product(bank[m][:, 0:REST], 0, 1, m, 1, lambda k: xhi[:, 0:REST], lambda k: xlo[:, 0:REST])
                        last.then_inc(s.r_l1, 1)
                        pe.wait_ge(s.r_g1l, n)
                        for m in range(MC):
                            last = product(bank[m][:, 0:REST], 0, 2, m, MC, lambda k: g1h[:, k, 0:REST],
                                           lambda k: g1l[:, k, 0:REST])
                        last.then_inc(s.r_l2, 1)
                        pe.wait_ge(s.r_g2l, n)
                        product(bank[4][:, 0:REST], 0, 3, 0, MC, lambda k: g2h[:, k, 0:REST],
                                lambda k: g2l[:, k, 0:REST]).then_inc(s.r_l3, 1)
                        pe.wait_ge(s.r_yT, n)
                        for j in range(RC):
                            last = t.transpose(bank[6][:, 128 * j:128 * j + D], yT[:, 128 * j:128 * j + 128], identf[:])
                        last.then_inc(s.r_y, 1)


NAMES = ["x", "ctx_1024", "L0_xattn_igate_w", "L0_xattn_igate_b", "L0_xattn_fgate_w", "L0_xattn_fgate_b",
         "L0_xattn_ln_scale", "L0_ffn_expert_tokens", "L0_ffn_W1", "L0_ffn_b1", "L0_ffn_W2", "L0_ffn_b2",
         "L0_ffn_W3", "L0_ffn_b3"]


def kernel(**inputs):
    import numpy as _np
    import concourse.bacc as _bacc
    from concourse import mybir as _mybir
    from concourse.bass_utils import run_bass_kernel_spmd as _run

    nc = _bacc.Bacc("TRN2", target_bir_lowering=False, num_devices=1)
    arrays, args = {}, []
    for name in NAMES:
        a = _np.ascontiguousarray(inputs[name])
        arrays[f"in_{name}"] = a
        args.append(nc.dram_tensor(f"in_{name}", a.shape, _mybir.dt.from_np(a.dtype), kind="ExternalInput").ap())
    out = nc.dram_tensor("out_rows", (T + PAD, D), F32, kind="ExternalOutput").ap()
    build(nc, *args, out)
    r = _run(nc, [arrays], core_ids=[0])
    return r.results[0]["out_rows"][0:T].reshape(B, S, D)
```
